# Optimizing a Trainium2 kernel written in Bass

```python
import numpy as np
import jax
import jax.numpy as jnp

def _softmax(x, axis=-1):
    return jax.nn.softmax(x, axis=axis)

def _gelu(x):
    return jax.nn.gelu(x, approximate=True)

def _silu(x):
    return jax.nn.silu(x)

def _sigmoid(x):
    return jax.nn.sigmoid(x)

def _layernorm(x, axis=-1, eps=1e-05):
    m = jnp.mean(x, axis=axis, keepdims=True)
    v = jnp.var(x, axis=axis, keepdims=True)
    return (x - m) / jnp.sqrt(v + eps)

def _scatter_add(tgt, idx, src, axis=0):
    return tgt.at[idx].add(src)

def _segment_sum(src, seg, n):
    return jax.ops.segment_sum(src, seg, n)
kernel_name = 'mk_sandwich_d2_jaxref_r8_5611af'

def setup_inputs(seed: int=0):
    np.random.seed(seed)
    _w = jnp.asarray

    def _L0_attn_setup():
        import jax, jax.numpy as jnp
        import numpy as np
        B, S, E, H, P = (2, 256, 128, 16, 256)
        HD = E // H
        key = jax.random.key(seed)
        ks = jax.random.split(key, 10)
        std = E ** (-0.5)
        x = jax.random.normal(ks[0], (B, S, E), jnp.float32)
        Wq = jax.random.normal(ks[1], (E, E), jnp.float32) * std
        Wk = jax.random.normal(ks[2], (E, E), jnp.float32) * std
        Wv = jax.random.normal(ks[3], (E, E), jnp.float32) * std
        Wo = jax.random.normal(ks[4], (E, E), jnp.float32) * std
        rel_key = jax.random.normal(ks[5], (P, HD), jnp.float32) * 0.02
        z = jnp.zeros((E,), jnp.float32)
        return {'x': x, 'Wq': Wq, 'bq': z, 'Wk': Wk, 'bk': z, 'Wv': Wv, 'bv': z, 'Wo': Wo, 'bo': z, 'rel_key': rel_key}
    _L0_attn_in = _L0_attn_setup()

    def _L0_ffn_setup():
        import jax, jax.numpy as jnp
        import numpy as np
        DIM = 128
        HIDDEN = 384
        SCALE = 1.0 / 127.0

        def _dequant(w_int, dtype):
            return w_int.astype(dtype) * jnp.asarray(SCALE, dtype)
        key = jax.random.key(seed)
        k_x, k_g, k_u, k_d = jax.random.split(key, 4)
        x = jax.random.normal(k_x, (4, 256, DIM), dtype=jnp.float32)
        w_gate = jax.random.randint(k_g, (HIDDEN, DIM), -127, 128, dtype=jnp.int32)
        w_up = jax.random.randint(k_u, (HIDDEN, DIM), -127, 128, dtype=jnp.int32)
        w_down = jax.random.randint(k_d, (DIM, HIDDEN), -127, 128, dtype=jnp.int32)
        return {'x': x, 'w_gate': w_gate, 'w_up': w_up, 'w_down': w_down}
    _L0_ffn_in = _L0_ffn_setup()

    def _L1_attn_setup():
        import jax, jax.numpy as jnp
        import numpy as np
        EMBED_DIM = 128
        NUM_HEADS = 16

        def quat_norm(q, eps=1e-06):
            r, i, j, k = jnp.split(q, 4, axis=-1)
            n = jnp.sqrt(r * r + i * i + j * j + k * k + eps)
            return jnp.concatenate([r / n, i / n, j / n, k / n], axis=-1)

        def quat_linear(x, W, b):
            B, T, D = x.shape
            D4 = D // 4
            xs = x.reshape(B, T, 4, D4)
            A = jnp.einsum('btcd,wdo->btcwo', xs, W) + b
            r = A[:, :, 0, 0] - A[:, :, 1, 1] - A[:, :, 2, 2] - A[:, :, 3, 3]
            i = A[:, :, 1, 0] + A[:, :, 0, 1] + A[:, :, 3, 2] - A[:, :, 2, 3]
            j = A[:, :, 2, 0] - A[:, :, 3, 1] + A[:, :, 0, 2] + A[:, :, 1, 3]
            k = A[:, :, 3, 0] + A[:, :, 2, 1] - A[:, :, 1, 2] + A[:, :, 0, 3]
            return jnp.concatenate([r, i, j, k], axis=-1)
        key = jax.random.key(seed)
        ks = jax.random.split(key, 10)
        B, T, D = (2, 256, EMBED_DIM)
        D4 = D // 4
        s = 0.02
        x = jax.random.normal(ks[0], (B, T, D), dtype=jnp.float32)

        def proj(kw, kb):
            W = jax.random.normal(kw, (4, D4, D4), dtype=jnp.float32) * s
            b = jax.random.normal(kb, (4, D4), dtype=jnp.float32) * s
            return (W, b)
        qW, qb = proj(ks[1], ks[2])
        kW, kb = proj(ks[3], ks[4])
        vW, vb = proj(ks[5], ks[6])
        oW, ob = proj(ks[7], ks[8])
        J = jax.random.normal(ks[9], (D,), dtype=jnp.float32) * 0.01
        return {'x': x, 'qW': qW, 'qb': qb, 'kW': kW, 'kb': kb, 'vW': vW, 'vb': vb, 'oW': oW, 'ob': ob, 'J': J}
    _L1_attn_in = _L1_attn_setup()

    def _L1_ffn_setup():
        import jax, jax.numpy as jnp
        import numpy as np
        NUM_EXPERTS = 8
        TOP_K = 2
        key = jax.random.key(seed)
        ks = jax.random.split(key, 6)
        B, S, D, F = (2, 256, 128, 512)
        E = NUM_EXPERTS
        sd = 1.0 / np.sqrt(D)
        sf = 1.0 / np.sqrt(F)
        return {'x': jax.random.normal(ks[0], (B, S, D), dtype=jnp.float32), 'gate_w': jax.random.normal(ks[1], (E, D), dtype=jnp.float32) * sd, 'w1': jax.random.uniform(ks[2], (F, E, D), dtype=jnp.float32, minval=-sd, maxval=sd), 'b1': jax.random.uniform(ks[3], (E, F), dtype=jnp.float32, minval=-sd, maxval=sd), 'w2': jax.random.uniform(ks[4], (D, E, F), dtype=jnp.float32, minval=-sf, maxval=sf), 'b2': jax.random.uniform(ks[5], (E, D), dtype=jnp.float32, minval=-sf, maxval=sf)}
    _L1_ffn_in = _L1_ffn_setup()
    _d = {'L0_attn_x': _L0_attn_in['x'], 'L0_attn_Wq': _L0_attn_in['Wq'], 'L0_attn_bq': _L0_attn_in['bq'], 'L0_attn_Wk': _L0_attn_in['Wk'], 'L0_attn_bk': _L0_attn_in['bk'], 'L0_attn_Wv': _L0_attn_in['Wv'], 'L0_attn_bv': _L0_attn_in['bv'], 'L0_attn_Wo': _L0_attn_in['Wo'], 'L0_attn_bo': _L0_attn_in['bo'], 'L0_attn_rel_key': _L0_attn_in['rel_key'], 'L0_ffn_w_gate': _L0_ffn_in['w_gate'], 'L0_ffn_w_up': _L0_ffn_in['w_up'], 'L0_ffn_w_down': _L0_ffn_in['w_down'], 'L1_attn_qW': _L1_attn_in['qW'], 'L1_attn_qb': _L1_attn_in['qb'], 'L1_attn_kW': _L1_attn_in['kW'], 'L1_attn_kb': _L1_attn_in['kb'], 'L1_attn_vW': _L1_attn_in['vW'], 'L1_attn_vb': _L1_attn_in['vb'], 'L1_attn_oW': _L1_attn_in['oW'], 'L1_attn_ob': _L1_attn_in['ob'], 'L1_attn_J': _L1_attn_in['J'], 'L1_ffn_gate_w': _L1_ffn_in['gate_w'], 'L1_ffn_w1': _L1_ffn_in['w1'], 'L1_ffn_b1': _L1_ffn_in['b1'], 'L1_ffn_w2': _L1_ffn_in['w2'], 'L1_ffn_b2': _L1_ffn_in['b2']}
    _x0 = _d['L0_attn_x']
    _d['L0_attn_x'] = jax.random.normal(jax.random.fold_in(jax.random.key(seed), 1), (4, 512, 128), dtype=_x0.dtype)
    del _x0
    return _d

def reference(L0_attn_x, L0_attn_Wq, L0_attn_bq, L0_attn_Wk, L0_attn_bk, L0_attn_Wv, L0_attn_bv, L0_attn_Wo, L0_attn_bo, L0_attn_rel_key, L0_ffn_w_gate, L0_ffn_w_up, L0_ffn_w_down, L1_attn_qW, L1_attn_qb, L1_attn_kW, L1_attn_kb, L1_attn_vW, L1_attn_vb, L1_attn_oW, L1_attn_ob, L1_attn_J, L1_ffn_gate_w, L1_ffn_w1, L1_ffn_b1, L1_ffn_w2, L1_ffn_b2):

    def _L0_attn_ref(x, Wq, bq, Wk, bk, Wv, bv, Wo, bo, rel_key):
        import jax, jax.numpy as jnp
        import numpy as np
        B, S, E, H, P = (2, 256, 128, 16, 256)
        HD = E // H
        b, s, e = x.shape
        p, hd = rel_key.shape
        h = e // hd
        scale = hd ** (-0.5)

        def split_heads(t):
            return t.reshape(b, s, h, hd).transpose(0, 2, 1, 3)
        q = split_heads(x @ Wq + bq)
        k = split_heads(x @ Wk + bk)
        v = split_heads(x @ Wv + bv)
        scores = jnp.einsum('bhid,bhjd->bhij', q, k)
        rel = jnp.einsum('bhid,pd->bhip', q, rel_key)
        i = jnp.arange(s)[:, None]
        j = jnp.arange(s)[None, :]
        rel_idx = jnp.clip(j - i + p - 1, 0, p - 1)
        bias = jnp.take_along_axis(rel, jnp.broadcast_to(rel_idx[None, None], (b, h, s, s)), axis=3)
        causal = j <= i
        logits = jnp.where(causal[None, None], (scores + bias) * scale, -jnp.inf)
        attn = jax.nn.softmax(logits, axis=-1)
        out = jnp.einsum('bhij,bhjd->bhid', attn, v)
        out = out.transpose(0, 2, 1, 3).reshape(b, s, e)
        return out @ Wo + bo

    def _L0_ffn_ref(x, w_gate, w_up, w_down):
        import jax, jax.numpy as jnp
        import numpy as np
        DIM = 128
        HIDDEN = 384
        SCALE = 1.0 / 127.0

        def _dequant(w_int, dtype):
            return w_int.astype(dtype) * jnp.asarray(SCALE, dtype)
        wg = _dequant(w_gate, x.dtype)
        wu = _dequant(w_up, x.dtype)
        wd = _dequant(w_down, x.dtype)
        gate = jnp.einsum('bsd,hd->bsh', x, wg)
        up = jnp.einsum('bsd,hd->bsh', x, wu)
        h = jax.nn.silu(gate) * up
        return jnp.einsum('bsh,dh->bsd', h, wd)

    def _L1_attn_ref(x, qW, qb, kW, kb, vW, vb, oW, ob, J):
        import jax, jax.numpy as jnp
        import numpy as np
        EMBED_DIM = 128
        NUM_HEADS = 16

        def quat_norm(q, eps=1e-06):
            r, i, j, k = jnp.split(q, 4, axis=-1)
            n = jnp.sqrt(r * r + i * i + j * j + k * k + eps)
            return jnp.concatenate([r / n, i / n, j / n, k / n], axis=-1)

        def quat_linear(x, W, b):
            B, T, D = x.shape
            D4 = D // 4
            xs = x.reshape(B, T, 4, D4)
            A = jnp.einsum('btcd,wdo->btcwo', xs, W) + b
            r = A[:, :, 0, 0] - A[:, :, 1, 1] - A[:, :, 2, 2] - A[:, :, 3, 3]
            i = A[:, :, 1, 0] + A[:, :, 0, 1] + A[:, :, 3, 2] - A[:, :, 2, 3]
            j = A[:, :, 2, 0] - A[:, :, 3, 1] + A[:, :, 0, 2] + A[:, :, 1, 3]
            k = A[:, :, 3, 0] + A[:, :, 2, 1] - A[:, :, 1, 2] + A[:, :, 0, 3]
            return jnp.concatenate([r, i, j, k], axis=-1)
        B, T, D = x.shape
        H = NUM_HEADS
        Dh = D // H
        scale = Dh ** (-0.5)
        q = quat_norm(quat_linear(x, qW, qb))
        k = quat_norm(quat_linear(x, kW, kb))
        v = quat_linear(x, vW, vb)
        q_ = q.reshape(B, T, H, Dh)
        k_ = k.reshape(B, T, H, Dh)
        v_ = v.reshape(B, T, H, Dh)
        scores = jnp.einsum('bthd,bshd->bhts', q_, k_) * scale
        scores = scores + jnp.mean(jnp.sin(J[:T])) * 0.1
        attn = jax.nn.softmax(scores, axis=-1)
        out = jnp.einsum('bhts,bshd->bthd', attn, v_).reshape(B, T, D)
        return quat_linear(out, oW, ob)

    def _L1_ffn_ref(x, gate_w, w1, b1, w2, b2):
        import jax, jax.numpy as jnp
        import numpy as np
        NUM_EXPERTS = 8
        TOP_K = 2
        logits = jnp.einsum('bsd,ed->bse', x, gate_w)
        probs = jax.nn.softmax(logits, axis=-1)
        topk_probs, topk_idx = jax.lax.top_k(probs, TOP_K)
        oh = jax.nn.one_hot(topk_idx, NUM_EXPERTS, dtype=x.dtype)
        h = jnp.einsum('bsd,fed,bske->bskf', x, w1, oh)
        h = h + jnp.take(b1, topk_idx, axis=0)
        h = jax.nn.gelu(h)
        y = jnp.einsum('bskf,def,bske->bskd', h, w2, oh)
        y = y + jnp.take(b2, topk_idx, axis=0)
        out = jnp.sum(y * topk_probs[..., None], axis=-2)
        return out
    x = L0_attn_x
    x = x + _layernorm(_L0_attn_ref(_layernorm(x, axis=-1), L0_attn_Wq, L0_attn_bq, L0_attn_Wk, L0_attn_bk, L0_attn_Wv, L0_attn_bv, L0_attn_Wo, L0_attn_bo, L0_attn_rel_key), axis=-1)
    x = x + _layernorm(_L0_ffn_ref(_layernorm(x, axis=-1), L0_ffn_w_gate, L0_ffn_w_up, L0_ffn_w_down), axis=-1)
    x = x + _layernorm(_L1_attn_ref(_layernorm(x, axis=-1), L1_attn_qW, L1_attn_qb, L1_attn_kW, L1_attn_kb, L1_attn_vW, L1_attn_vb, L1_attn_oW, L1_attn_ob, L1_attn_J), axis=-1)
    x = x + _layernorm(_L1_ffn_ref(_layernorm(x, axis=-1), L1_ffn_gate_w, L1_ffn_w1, L1_ffn_b1, L1_ffn_w2, L1_ffn_b2), axis=-1)
    return x

_drawn_inputs = setup_inputs


def setup_inputs(seed=0):
    import zlib

    import numpy as np

    out = dict(_drawn_inputs(seed))
    spreads = {'L0_attn_bq': (0.0, 0.1),
     'L0_attn_bk': (0.0, 0.8),
     'L0_attn_bv': (0.0, 0.1),
     'L0_attn_bo': (0.0, 0.1)}
    factors = {'L1_attn_qb': 4.001, 'L1_attn_kb': 4.626, 'L1_attn_J': 8.0}
    for name, (base, spread) in spreads.items():
        noise = np.random.default_rng([zlib.crc32(name.encode()), seed]).standard_normal(out[name].shape)
        drawn = base * np.exp(spread * noise) if base else spread * noise
        out[name] = jnp.asarray(drawn.astype(out[name].dtype))
    for name, factor in factors.items():
        out[name] = (out[name] * factor).astype(out[name].dtype)
    return out
```

```python
import numpy as np
import concourse.bass as bass
from concourse import mybir
from contextlib import ExitStack


class Signal:

    def __init__(self, sem, per, base=0):
        self.sem, self.per, self.base = sem, per, base

    def at(self, batch, n):
        return batch * self.per + (self.base + n)


def build_sandwich(nc, X, Wq, bq, Wk, bk, Wv, bv, Wo, bo, rel_key, w_gate, w_up, w_down,
                   qW, qb, kW, kb, vW, vb, oW, ob, J, gate_w, w1, b1, w2, b2, out):
    f32, i32, u32 = mybir.dt.float32, mybir.dt.int32, mybir.dt.uint32
    ALU = mybir.AluOpType
    ACT = mybir.ActivationFunctionType
    AXX = mybir.AxisListType.X

    B, S, E = X.shape
    P = 128
    T = S // P
    NREL, D = rel_key.shape
    H = E // D
    QB = P // H
    NQB = S // QB
    QPT = P // QB
    RR = QB * D
    HID = w_gate.shape[0]
    FT = HID // P
    NF, NE, _ = w1.shape
    MF = NF // P
    QD = E // 4
    SCALE = float(D) ** -0.5
    DEQ = 1.0 / 127.0
    LN_EPS, QN_EPS = 1e-5, 1e-6
    MASKED = -1e30
    TWO_PI = 2.0 * np.pi
    NB = 4

    ctx = ExitStack()
    with ctx:
        nc.disable_value_cache = True

        def sb(name, shape, dt=f32):
            return ctx.enter_context(nc.sbuf_tensor(name, shape, dt))

        def sem(name):
            return ctx.enter_context(nc.semaphore(name))

        ident = sb("ident", [P, P])
        ones = sb("ones", [1, P])
        head_mask = sb("head_mask", [P, H])
        query_mask = sb("query_mask", [P, QB])
        same_part = sb("same_part", [P, P])
        signs = sb("signs", [P, 4])
        eps_col = sb("eps_col", [P, 2])
        spare = sb("spare", [P, 4])
        expert_no = sb("expert_no", [P, NE])
        toep = sb("toep", [RR + QB, S])
        rel_rows = sb("rel_rows", [RR, NREL])
        w_qkvo = sb("w_qkvo", [P, 4, P])
        q_bias = sb("q_bias", [P, 1])
        k_bias = sb("k_bias", [P, 1])
        wq_rep = sb("wq_rep", [P, H // 2, 2, QB, D])
        q_bias_rep = sb("q_bias_rep", [P, H // 2])
        bias_rows = sb("bias_rows", [1, 2, P])
        rel_in = sb("rel_in", [P, NREL // P, D])
        wgT = sb("wgT", [P, HID])
        wuT = sb("wuT", [P, HID])
        wdT = sb("wdT", [P, FT, P])
        w_quat = sb("w_quat", [P, 4, 4, QD])
        qbias_in = sb("qbias_in", [1, 4, 4, QD])
        qbias_row = sb("qbias_row", [1, 4, 4, QD])
        qbias_col = sb("qbias_col", [P, 2])
        j_row = sb("j_row", [1, P])
        j_turn = sb("j_turn", [1, P])
        j_sum = sb("j_sum", [1, 1])
        j_bias = sb("j_bias", [P, 1])
        w1T = sb("w1T", [P, NE, NF])
        w2T = sb("w2T", [P, MF, NE, P])
        gateT = sb("gateT", [P, NE])
        b1T = sb("b1T", [P, MF, NE])
        b2_sb = sb("b2_sb", [NE, P])
        x_in = sb("x_in", [P, T, E])
        x = sb("x", [P, T, E])
        x_out = sb("x_out", [P, T, E])
        stats = sb("stats", [P, T, 6])
        moments = sb("moments", [P, T, 2])
        rstd = sb("rstd", [P, T])
        xn = sb("xn", [P, T, E])
        xnT = sb("xnT", [P, S])
        qT = sb("qT", [P, S])
        kT = sb("kT", [P, S])
        v_ones = sb("v_ones", [P, T, H, D + 1])
        q_wide = sb("q_wide", [P, NQB * H * QB])
        q_rel = sb("q_rel", [RR + QB, NQB, H, QB])
        probs = sb("probs", [P, NB, S])
        pT_all = sb("pT_all", [P, (2 * T - 1) * H * P])
        neg_max = sb("neg_max", [P, 8])
        den = sb("den", [P, T, H])
        attn = xn
        attnT = xnT
        q_wide0 = q_wide[:].rearrange("p (n h i) -> p n h i", h=H, i=QB)
        q_wide2 = q_wide[:].rearrange("p (h s) -> p h s", h=H)
        pT_flat = pT_all[:]
        pT_odd = (T - 1) * H * P
        probsT = [pT_flat[:, 0:pT_odd].rearrange("p (c h i) -> p c h i", c=T - 1, h=H),
                  pT_flat[:, pT_odd:].rearrange("p (c h i) -> p c h i", c=T, h=H)]
        w1_in = pT_flat[:, 0:MF * NE * P].rearrange("p (m e d) -> p m e d", m=MF, e=NE)
        w2_in = pT_flat[:, MF * NE * P:2 * MF * NE * P].rearrange("p (e f) -> p e f", e=NE)
        o0 = 2 * MF * NE * P
        wi_in = pT_flat[:, o0:o0 + 3 * HID].bitcast(i32).rearrange("p (w n) -> p w n", w=3)
        wf_in = pT_flat[:, o0 + 3 * HID:o0 + 6 * HID].rearrange("p (w n) -> p w n", w=3)
        b1_in = pT_flat[0:NE, o0 + 6 * HID:o0 + 6 * HID + NF]
        gate_in = pT_flat[0:NE, o0 + 6 * HID + NF:o0 + 6 * HID + NF + P]
        rel_rep = pT_flat[:, o0 + 6 * HID + NF + P:o0 + 6 * HID + NF + P + RR * NREL // P].rearrange(
            "p (a i d) -> p a i d", a=NREL // P, i=QB)
        head_probs = pT_flat[:, 0:2 * T * S].rearrange("p (a t s) -> p a t s", a=2, t=T)
        lin = pT_flat[:, 2 * T * S:2 * T * S + 2 * S].rearrange("p (w s) -> p w s", w=2)
        lin_sq = pT_flat[:, 2 * T * S + 2 * S:2 * T * S + 4 * S].rearrange("p (w s) -> p w s", w=2)
        hid_e = pT_flat[:, 0:FT * S].rearrange("p (f s) -> p f s", f=FT)
        hid = pT_flat[:, FT * S:2 * FT * S].rearrange("p (f s) -> p f s", f=FT)
        moe_h = pT_flat[:, 0:2 * MF * S].rearrange("p (a f s) -> p a f s", a=2, f=MF)
        acc = pT_flat[:, 2 * MF * S:2 * MF * S + T * E].rearrange("p (t d) -> p t d", t=T)
        router = sb("router", [P, T, NE])
        router_e = sb("router_e", [P, T, NE])
        router_s = sb("router_s", [P, T, 2])
        top8 = sb("top8", [P, T, 8])
        top_idx = sb("top_idx", [P, T, 8], u32)
        top_idx_f = sb("top_idx_f", [P, T, 8])
        gates = sb("gates", [P, T, NE])
        gates2 = sb("gates2", [P, T, NE])
        gates_T = sb("gates_T", [NE, T, P])

        ps = ctx.enter_context(nc.psum_tensor("ps", [P, 8, 512], f32))

        ld_attn, ld_ffn, ld_quat, ld_moe = sem("ld_attn"), sem("ld_ffn"), sem("ld_quat"), sem("ld_moe")
        toep_dma = sem("toep_dma")
        pool_step = sem("pool_step")
        consts_ready = sem("consts_ready")
        prep_done = sem("prep_done")
        prep_act = sem("prep_act")
        prep_dve = sem("prep_dve")
        rep_ready = sem("rep_ready")
        wf_ready = sem("wf_ready")
        prep_chain = sem("prep_chain")
        j_ready = sem("j_ready")
        toep_base = sem("toep_base")
        qb_ready = sem("qb_ready")
        x_loaded = Signal(sem("x_loaded"), 16)
        x_copied = Signal(sem("x_copied"), 1, base=1)
        x_final = Signal(sem("x_final"), 1, base=1)
        x_stored = Signal(sem("x_stored"), 16, base=16)
        dve_step = Signal(sem("dve_step"), 42)
        xn_ready = Signal(sem("xn_ready"), 4 * T)
        xnT_ps = Signal(sem("xnT_ps"), 4)
        xnT_ready = Signal(sem("xnT_ready"), 4)
        y_ready = Signal(sem("y_ready"), 3)
        proj_ps = Signal(sem("proj_ps"), 6)
        proj_copied = Signal(sem("proj_copied"), 8)
        qrel_ps = Signal(sem("qrel_ps"), H // 2)
        qrel_ready = Signal(sem("qrel_ready"), H // 2)
        qwide_ready = Signal(sem("qwide_ready"), T)
        probs_zero = Signal(sem("probs_zero"), 1)
        scores_ready = Signal(sem("scores_ready"), NQB)
        max_ready = Signal(sem("max_ready"), NQB)
        exp_ready = Signal(sem("exp_ready"), NQB)
        pT_ps = Signal(sem("pT_ps"), NQB)
        pT_dve = Signal(sem("pT_dve"), NQB // 2)
        pT_act = Signal(sem("pT_act"), NQB // 2)
        av_ps = Signal(sem("av_ps"), T)
        attn_ready = Signal(sem("attn_ready"), T + 2)
        attnT_ps = Signal(sem("attnT_ps"), T + 1)
        attnT_ready = Signal(sem("attnT_ready"), T + 1)
        gu_ps = Signal(sem("gu_ps"), 2 * FT)
        ge_ready = Signal(sem("ge_ready"), FT)
        hid_ready = Signal(sem("hid_ready"), FT)
        norm_ps = Signal(sem("norm_ps"), 2)
        qnorm_ready = Signal(sem("qnorm_ready"), 2)
        var_ready = Signal(sem("var_ready"), 8)
        rstd_ready = Signal(sem("rstd_ready"), 8)
        act_step = Signal(sem("act_step"), 10)
        qk_ready = Signal(sem("qk_ready"), 2)
        qwide2_ready = Signal(sem("qwide2_ready"), H)
        s2_ready = Signal(sem("s2_ready"), 2 * H)
        e2_ready = Signal(sem("e2_ready"), 2 * H)
        av2_ps = Signal(sem("av2_ps"), H)
        router_ps = Signal(sem("router_ps"), 1)
        router_in = Signal(sem("router_in"), 1)
        router_exp = Signal(sem("router_exp"), 1)
        gates_ready = Signal(sem("gates_ready"), 1)
        gatesT_ps = Signal(sem("gatesT_ps"), 1)
        gatesT_ready = Signal(sem("gatesT_ready"), 1)
        accb_ps = Signal(sem("accb_ps"), 1)
        moe_h_ps = Signal(sem("moe_h_ps"), NE * MF)
        moe_h_ready = Signal(sem("moe_h_ready"), NE * MF)
        moe_y_ps = Signal(sem("moe_y_ps"), NE)
        moe_y_used = Signal(sem("moe_y_used"), NE)

        MATS = [qW, kW, vW, oW]
        QBIAS = [qb, kb, vb, ob]
        PREP_BANKS = 8

        block = ctx.enter_context(nc.Block())

        @block.sync
        def _(sp):
            n = 0
            for j, w in enumerate((Wq, Wk, Wv, Wo)):
                sp.dma_start(w_qkvo[:, j, :], w).then_inc(ld_attn, 16)
            sp.dma_start(q_bias[:], bq.rearrange("(p a) -> p a", a=1)).then_inc(ld_attn, 16)
            sp.dma_start(k_bias[:], bk.rearrange("(p a) -> p a", a=1)).then_inc(ld_attn, 16)
            sp.dma_start(bias_rows[:, 0, :], bv.rearrange("(a p) -> a p", a=1)).then_inc(ld_attn, 16)
            sp.dma_start(bias_rows[:, 1, :], bo.rearrange("(a p) -> a p", a=1)).then_inc(ld_attn, 16)
            sp.dma_start(rel_in[:], rel_key.rearrange("(a p) d -> p a d", p=P)).then_inc(ld_attn, 16)
            for hh in range(2):
                for i in range(QB):
                    r = hh * RR + i * D
                    sp.dma_start(q_bias_rep[r:r + D, :],
                                 bq.rearrange("(c z d) -> z d c", z=2, d=D)[hh],
                                 allow_slow_non_contiguous=True).then_inc(ld_attn, 16)
            sp.dma_start(wi_in[:, 0, :].rearrange("p (f d) -> p f d", f=FT),
                         w_gate.rearrange("(f p) d -> p f d", p=P)).then_inc(ld_ffn, 16)
            sp.dma_start(wi_in[:, 1, :].rearrange("p (f d) -> p f d", f=FT),
                         w_up.rearrange("(f p) d -> p f d", p=P)).then_inc(ld_ffn, 16)
            sp.dma_start(wi_in[:, 2, :], w_down).then_inc(ld_ffn, 16)
            sp.dma_start(w1_in, w1.rearrange("(m p) e d -> p m e d", p=P)).then_inc(ld_moe, 16)
            sp.dma_start(w2_in, w2).then_inc(ld_moe, 16)
            sp.wait_ge(toep_base, 2)
            for i in range(QB):
                c = S - QB - NREL + 1 + i
                sp.dma_start(toep[i * D:(i + 1) * D, c:c + NREL],
                             rel_rows[i * D:(i + 1) * D, :]).then_inc(toep_dma, 16)
            with sp.Fori(0, B) as b:
                sp.wait_ge(x_copied.sem, x_copied.at(b, 0))
                sp.dma_start(x_in[:], X[bass.ds(b, 1)].rearrange("a (t p) e -> p (a t) e", p=P)
                             ).then_inc(x_loaded.sem, 16)
            sp.wait_ge(x_stored.sem, 16 * (B + 1))

        @block.gpsimd
        def _(pool):
            done = [0]

            def step(ins):
                done[0] += 1
                ins.then_inc(pool_step, 1)
                pool.wait_ge(pool_step, done[0])

            step(pool.memset(ident[:], 0.0))
            step(pool.affine_select(out=ident[:], in_=ident[:], compare_op=ALU.not_equal, fill=1.0,
                                    base=0, pattern=[[-1, P]], channel_multiplier=1))
            step(pool.memset(ones[:], 1.0))
            step(pool.memset(eps_col[:, 0:1], LN_EPS))
            step(pool.memset(eps_col[:, 1:2], QN_EPS))
            step(pool.memset(head_mask[:], SCALE))
            step(pool.affine_select(out=head_mask[:], in_=head_mask[:], compare_op=ALU.is_ge, fill=0.0,
                                    base=0, pattern=[[-D, H]], channel_multiplier=1))
            step(pool.affine_select(out=head_mask[:], in_=head_mask[:], compare_op=ALU.is_ge, fill=0.0,
                                    base=D - 1, pattern=[[D, H]], channel_multiplier=-1))
            step(pool.memset(query_mask[:], SCALE))
            for r in (0, RR):
                m = query_mask[r:r + RR, :]
                step(pool.affine_select(out=m, in_=m, compare_op=ALU.is_ge, fill=0.0,
                                        base=0, pattern=[[-D, QB]], channel_multiplier=1))
                step(pool.affine_select(out=m, in_=m, compare_op=ALU.is_ge, fill=0.0,
                                        base=D - 1, pattern=[[D, QB]], channel_multiplier=-1))
            step(pool.memset(same_part[:], 0.0))
            for k in range(-3, 4):
                step(pool.affine_select(out=same_part[:], in_=same_part[:], compare_op=ALU.not_equal, fill=1.0,
                                        base=k * QD, pattern=[[-1, P]], channel_multiplier=1))
            step(pool.memset(signs[:], 1.0))
            for c, part in ((1, 0), (2, 0), (3, 0), (2, 1), (3, 2), (1, 3)):
                step(pool.memset(signs[c * QD:(c + 1) * QD, part:part + 1], -1.0))
            step(pool.iota(expert_no[:], [[1, NE]], base=0, channel_multiplier=0,
                           allow_small_or_imprecise_dtypes=True))
            step(pool.memset(v_ones[:], 1.0))
            step(pool.memset(toep[RR:RR + QB, :], 0.0))
            step(pool.affine_select(out=toep[RR:RR + QB, :], in_=toep[RR:RR + QB, :], compare_op=ALU.is_ge,
                                    fill=MASKED, base=S - QB, pattern=[[-1, S]], channel_multiplier=1))
            rows = q_rel[RR:RR + QB, :, :, :].rearrange("p n h i -> p (n h) i")
            step(pool.memset(rows, 0.0))
            pool.affine_select(out=rows, in_=rows, compare_op=ALU.not_equal, fill=1.0, base=0,
                               pattern=[[0, NQB * H], [-1, QB]], channel_multiplier=1
                               ).then_inc(consts_ready, 1)

            with pool.Fori(0, B) as b:
                pool.wait_ge(proj_copied.sem, proj_copied.at(b, 1))
                for t in range(T):
                    if t == 1:
                        pool.memset(probs[:], 0.0).then_inc(probs_zero.sem, 1)
                    blocks = slice(t * QPT, (t + 1) * QPT)
                    q_in = qT[:, t * P:(t + 1) * P].rearrange("p (n i) -> p n i", i=QB)
                    pool.tensor_tensor(
                        out=q_wide0[:, blocks, :, :],
                        in0=q_in.unsqueeze(2).broadcast_to([P, QPT, H, QB]),
                        in1=head_mask[:].unsqueeze(1).unsqueeze(3).broadcast_to([P, QPT, H, QB]),
                        op=ALU.mult).then_inc(qwide_ready.sem, 1)

        def prep_groups():
            yield ("rel", None)
            yield ("gate_up", 0)
            yield ("gate_up", 1)
            yield ("down", 2)
            yield ("small", None)
            for e in range(NE):
                yield ("w1", e)
                yield ("w2", e)
        groups = list(prep_groups())
        first_moe = 4

        def prep_copy(eng, copy, which):
            for n, (kind, a) in enumerate(groups):
                if n % 2 != which:
                    continue
                eng.wait_ge(prep_done, n + 1)
                bank = ps[:, n % PREP_BANKS, :]
                if kind == "rel":
                    last = copy(rel_rows[:], bank[0:RR, 0:NREL])
                elif kind == "gate_up":
                    last = copy((wgT, wuT)[a][:], bank[:, 0:HID])
                elif kind == "down":
                    last = copy(wdT[:], bank[:, 0:FT * P].rearrange("p (f d) -> p f d", f=FT))
                elif kind == "small":
                    copy(gateT[:], bank[:, 0:NE])
                    last = copy(b1T[:], bank[:, NE:NE + MF * NE].rearrange("p (m e) -> p m e", m=MF))
                elif kind == "w1":
                    last = copy(w1T[:, a, :], bank[:, :])
                else:
                    last = copy(w2T[:, :, a, :], bank[:, :].rearrange("p (m d) -> p m d", m=MF))
                last.then_inc((prep_act, prep_dve)[which], 1)

        def copies(n):
            return (n // 2 + 1, 0) if n % 2 == 0 else (0, n // 2 + 1)

        @block.scalar
        def _(act):
            for m, w in enumerate(MATS):
                for c in range(4):
                    for part in range(4):
                        act.dma_start(w_quat[c * QD:(c + 1) * QD, m, part, :], w[c ^ part]
                                      ).then_inc(ld_quat, 16)
            for m, w in enumerate(QBIAS):
                act.dma_start(qbias_in[:, m, :, :], w.rearrange("(a w) o -> a w o", a=1)).then_inc(ld_quat, 16)
            act.dma_start(j_row[:], J.rearrange("(a p) -> a p", a=1)).then_inc(ld_quat, 16)
            act.dma_start(gate_in, gate_w).then_inc(ld_moe, 16)
            act.dma_start(b1_in, b1).then_inc(ld_moe, 16)
            act.dma_start(b2_sb[:], b2).then_inc(ld_moe, 16)

            prep_copy(act, lambda o, i: nc.scalar.activation(o, i, ACT.Copy), 0)
            act.wait_ge(consts_ready, 1)
            act.wait_ge(j_ready, 1)
            nc.scalar.activation(j_turn[:], j_row[:], ACT.Sin, accum_out=j_sum[:]).then_inc(j_ready, 1)
            act.wait_ge(j_ready, 3)
            nc.scalar.mul(j_bias[:], ps[:, 7, 0:1], 0.1 / E).then_inc(j_ready, 1)
            nc.scalar.activation(qbias_col[:], ps[:, 7, 2:4], ACT.Copy).then_inc(j_ready, 1)

            with act.Fori(0, B) as b:
                norms, logs = [0], [0]

                def inv_sqrt(dst, src, eps):
                    logs[0] += 1
                    nc.scalar.activation(dst, src, ACT.Ln, bias=eps).then_inc(act_step.sem, 1)
                    act.wait_ge(act_step.sem, act_step.at(b, logs[0]))
                    return nc.scalar.activation(dst, dst, ACT.Exp, scale=-0.5)

                def token_rstd():
                    norms[0] += 1
                    act.wait_ge(var_ready.sem, var_ready.at(b, norms[0]))
                    inv_sqrt(rstd[:], moments[:, :, 1], eps_col[:, 0:1]).then_inc(rstd_ready.sem, 1)

                def transposed(k):
                    token_rstd()
                    act.wait_ge(xnT_ps.sem, xnT_ps.at(b, k + 1))
                    nc.scalar.activation(xnT[:], ps[:, 6, :], ACT.Copy).then_inc(xnT_ready.sem, 1)

                transposed(0)
                act.wait_ge(proj_ps.sem, proj_ps.at(b, 1))
                nc.scalar.activation(qT[:], ps[:, 0, :], ACT.Identity, bias=q_bias[:]
                                     ).then_inc(proj_copied.sem, 1)
                act.wait_ge(proj_ps.sem, proj_ps.at(b, 2))
                nc.scalar.activation(kT[:], ps[:, 1, :], ACT.Identity, bias=k_bias[:]
                                     ).then_inc(proj_copied.sem, 1)
                act.wait_ge(proj_ps.sem, proj_ps.at(b, 3))
                nc.scalar.activation(v_ones[:, :, :, 0:D],
                                     ps[:, 2, :].rearrange("p (t h d) -> p t h d", t=T, d=D),
                                     ACT.Copy).then_inc(proj_copied.sem, 1)
                act.wait_ge(probs_zero.sem, probs_zero.at(b, 1))

                def copy_pT(n):
                    act.wait_ge(pT_ps.sem, pT_ps.at(b, n + 1))
                    t, c = n // QPT, n // QPT + 1
                    if t >= 2:
                        act.wait_ge(av_ps.sem, av_ps.at(b, t - 1))
                    nc.scalar.activation(
                        probsT[t % 2][:, 0:c, :, (n % QPT) * QB:(n % QPT + 1) * QB],
                        ps[:, 4 + n % 2, 0:c * P].rearrange("p (c h i) -> p c h i", h=H, i=QB),
                        ACT.Copy).then_inc(pT_act.sem, 1)

                def copy_attnT(t):
                    act.wait_ge(attnT_ps.sem, attnT_ps.at(b, t + 1))
                    nc.scalar.activation(attnT[:, t * P:(t + 1) * P], ps[:, 6, 256:256 + P], ACT.Copy
                                         ).then_inc(attnT_ready.sem, 1)

                for n in range(NQB):
                    act.wait_ge(max_ready.sem, max_ready.at(b, n + 1))
                    if n >= NB:
                        act.wait_ge(pT_ps.sem, pT_ps.at(b, n - NB + 1))
                    L = QB * (n + 1)
                    nc.scalar.activation(probs[:, n % NB, 0:L], ps[:, n % NB, 0:L], ACT.Exp,
                                         bias=neg_max[:, n % 8:n % 8 + 1]).then_inc(exp_ready.sem, 1)
                    if n >= 2 and (n - 2) % 2:
                        copy_pT(n - 2)
                    if n >= QPT and n % QPT == 6:
                        copy_attnT(n // QPT - 1)
                copy_pT(NQB - 1)
                copy_attnT(T - 1)

                token_rstd()

                transposed(1)
                for f in range(FT):
                    act.wait_ge(gu_ps.sem, gu_ps.at(b, 2 * f + 1))
                    nc.scalar.activation(hid_e[:, f, :], ps[:, f, :], ACT.Exp, scale=-1.0
                                         ).then_inc(ge_ready.sem, 1)

                token_rstd()

                transposed(2)
                for w in range(2):
                    act.wait_ge(proj_ps.sem, proj_ps.at(b, 3 + w + 1))
                    nc.scalar.activation(lin[:, w, :], ps[:, w, :], ACT.Identity,
                                         bias=qbias_col[:, w:w + 1]).then_inc(proj_copied.sem, 1)
                    nc.scalar.activation(lin_sq[:, w, :], ps[:, w, :], ACT.Square,
                                         bias=qbias_col[:, w:w + 1]).then_inc(proj_copied.sem, 1)
                act.wait_ge(proj_ps.sem, proj_ps.at(b, 6))
                nc.scalar.activation(v_ones[:, :, :, 0:D],
                                     ps[:, 2, :].rearrange("p (t h d) -> p t h d", t=T, d=D),
                                     ACT.Copy).then_inc(proj_copied.sem, 1)
                for w in range(2):
                    act.wait_ge(norm_ps.sem, norm_ps.at(b, w + 1))
                    inv_sqrt(lin_sq[:, w, :], ps[:, 3 + w, :], eps_col[:, 1:2]).then_inc(qnorm_ready.sem, 1)
                for h in range(H):
                    for a in range(2):
                        act.wait_ge(s2_ready.sem, s2_ready.at(b, 2 * h + a + 1))
                        if h >= 2:
                            act.wait_ge(av2_ps.sem, av2_ps.at(b, h - 1))
                        nc.scalar.activation(head_probs[:, h % 2, 2 * a:2 * a + 2, :],
                                             ps[:, 2 * a:2 * a + 2, :], ACT.Exp, bias=j_bias[:]
                                             ).then_inc(e2_ready.sem, 1)
                act.wait_ge(attnT_ps.sem, attnT_ps.at(b, T + 1))
                nc.scalar.activation(attnT[:], ps[:, 6, :], ACT.Copy).then_inc(attnT_ready.sem, 1)

                token_rstd()

                transposed(3)
                act.wait_ge(router_in.sem, router_in.at(b, 1))
                nc.scalar.activation(router_e[:], router[:], ACT.Exp).then_inc(router_exp.sem, 1)
                act.wait_ge(gatesT_ps.sem, gatesT_ps.at(b, 1))
                nc.scalar.activation(gates_T[:], ps[0:NE, 7, :].rearrange("p (t s) -> p t s", t=T), ACT.Copy
                                     ).then_inc(gatesT_ready.sem, 1)
                for e in range(NE):
                    for m in range(MF):
                        n = e * MF + m
                        act.wait_ge(moe_h_ps.sem, moe_h_ps.at(b, n + 1))
                        if e >= 2 and m == 0:
                            act.wait_ge(moe_y_ps.sem, moe_y_ps.at(b, e - 1))
                        nc.scalar.activation(moe_h[:, e % 2, m, :], ps[:, n % NB, :], ACT.Gelu_apprx_tanh,
                                             bias=b1T[:, m, e:e + 1]).then_inc(moe_h_ready.sem, 1)
                token_rstd()
                assert norms[0] == var_ready.per and logs[0] == act_step.per
                act.wait_ge(x_final.sem, x_final.at(b, 1))
                act.dma_start(out[bass.ds(b, 1)].rearrange("a (t p) e -> p (a t) e", p=P), x_out[:]
                              ).then_inc(x_stored.sem, 16)

        @block.vector
        def _(dve):
            chain = [0]

            def prep(ins):
                chain[0] += 1
                ins.then_inc(prep_chain, 1)
                dve.wait_ge(prep_chain, chain[0])

            dve.wait_ge(ld_attn, (9 + 2 * QB) * 16)
            nc.vector.tensor_copy(rel_rep, rel_in[:].unsqueeze(2).broadcast_to([P, NREL // P, QB, D])
                                  ).then_inc(rep_ready, 1)
            for z in range(2):
                nc.vector.tensor_copy(wq_rep[:, :, z, :, :],
                                      w_qkvo[:, 0, :].rearrange("p (c z d) -> p c z d", z=2, d=D)[:, :, z, :]
                                      .unsqueeze(2).broadcast_to([P, H // 2, QB, D])).then_inc(rep_ready, 1)
            dve.wait_ge(ld_ffn, 3 * 16)
            nc.vector.tensor_scalar(wf_in, wi_in, DEQ, None, ALU.mult).then_inc(wf_ready, 1)
            prep_copy(dve, lambda o, i: nc.vector.tensor_copy(o, i), 1)
            dve.wait_ge(prep_act, 1)
            nc.vector.tensor_copy(toep[0:RR, 0:NREL], rel_rows[:, 0:1].broadcast_to([RR, NREL])
                                  ).then_inc(toep_base, 1)
            nc.vector.tensor_copy(toep[0:RR, NREL:S], rel_rows[:, NREL - 1:NREL].broadcast_to([RR, S - NREL])
                                  ).then_inc(toep_base, 1)
            dve.wait_ge(ld_quat, (4 * 16 + 5) * 16)
            dve.wait_ge(consts_ready, 1)
            wq_all = w_quat[:].rearrange("p m c o -> p m (c o)")
            for m in range(4):
                nc.vector.tensor_tensor(out=w_quat[:, m, :, :], in0=w_quat[:, m, :, :],
                                        in1=signs[:].unsqueeze(2).broadcast_to([P, 4, QD]),
                                        op=ALU.mult).then_inc(qb_ready, 1)
            SIGN = {0: "+---", 1: "+++-", 2: "+-++", 3: "++-+"}
            for w in range(1, 4):
                for part in range(4):
                    src = qbias_in[:, :, 0, :] if w == 1 else qbias_row[:, :, part, :]
                    ins = nc.vector.tensor_tensor(out=qbias_row[:, :, part, :], in0=src,
                                                  in1=qbias_in[:, :, w, :],
                                                  op=ALU.add if SIGN[part][w] == "+" else ALU.subtract)
                    if w < 3:
                        prep(ins)
                    else:
                        ins.then_inc(qb_ready, 1)
            BIG = 1.5 * 2.0 ** 23
            c1 = 6.28125
            c2 = float(np.float32(TWO_PI - c1))
            prep(nc.vector.tensor_scalar(j_turn[:], j_row[:], 1.0 / TWO_PI, BIG, ALU.mult, ALU.add))
            prep(nc.vector.tensor_scalar(j_turn[:], j_turn[:], BIG, None, ALU.subtract))
            prep(nc.vector.scalar_tensor_tensor(out=j_row[:], in0=j_turn[:], scalar=-c1, in1=j_row[:],
                                                op0=ALU.mult, op1=ALU.add))
            prep(nc.vector.scalar_tensor_tensor(out=j_row[:], in0=j_turn[:], scalar=-c2, in1=j_row[:],
                                                op0=ALU.mult, op1=ALU.add))
            PI_IN = float(np.nextafter(np.float32(np.pi), np.float32(0)))
            nc.vector.tensor_scalar(j_row[:], j_row[:], PI_IN, -PI_IN, ALU.min, ALU.max).then_inc(j_ready, 1)
            dve.wait_ge(j_ready, 5)
            nc.vector.memset(spare[:, 1:2], 0.0).then_inc(x_copied.sem, 1)
            nc.vector.memset(spare[:, 2:3], 0.0).then_inc(x_final.sem, 1)
            nc.vector.memset(spare[:, 3:4], 0.0).then_inc(x_stored.sem, 16)

            with dve.Fori(0, B) as b:
                count, norms = [0], [0]

                def step(ins):
                    count[0] += 1
                    ins.then_inc(dve_step.sem, 1)
                    dve.wait_ge(dve_step.sem, dve_step.at(b, count[0]))

                def carry_wait():
                    nc.vector.tensor_copy(spare[:, 0:1], ident[:, 0:1])

                def moments_of(src):
                    for t in range(T):
                        last = nc.vector.bn_stats(stats[:, t, :], src[:, t, :])
                    step(last)
                    carry_wait()
                    for t in range(T):
                        last = nc.vector.bn_aggr(moments[:, t, :], stats[:, t, :])
                    last.then_inc(var_ready.sem, 1)
                    norms[0] += 1
                    dve.wait_ge(rstd_ready.sem, rstd_ready.at(b, norms[0]))

                def norm_in(k):
                    moments_of(x)
                    for t in range(T):
                        nc.vector.tensor_scalar(xn[:, t, :], x[:, t, :], moments[:, t, 0:1], rstd[:, t:t + 1],
                                                ALU.subtract, ALU.mult).then_inc(xn_ready.sem, 1)

                def norm_out(y, dst):
                    moments_of(y)
                    for t in range(T):
                        last = nc.vector.tensor_scalar(xn[:, t, :], y[:, t, :], moments[:, t, 0:1],
                                                       rstd[:, t:t + 1], ALU.subtract, ALU.mult)
                    step(last)
                    return nc.vector.tensor_tensor(out=dst[:], in0=x[:], in1=xn[:], op=ALU.add)

                y_bank = ps[:, 7, :].rearrange("p (t e) -> p t e", t=T)

                dve.wait_ge(x_loaded.sem, x_loaded.at(b, 16))
                dve.wait_ge(x_final.sem, x_final.at(b, 0))
                nc.vector.tensor_copy(x[:], x_in[:]).then_inc(x_copied.sem, 1)
                dve.wait_ge(x_copied.sem, x_copied.at(b, 1))
                norm_in(0)
                for c in range(H // 2):
                    dve.wait_ge(qrel_ps.sem, qrel_ps.at(b, c + 1))
                    for hh in range(2):
                        rows = slice(hh * RR, (hh + 1) * RR)
                        last = nc.vector.scalar_tensor_tensor(
                            out=q_rel[0:RR, :, 2 * c + hh, :],
                            in0=ps[rows, 3 + c % 3, :].rearrange("p (n i) -> p n i", i=QB),
                            scalar=q_bias_rep[rows, c:c + 1],
                            in1=query_mask[rows, :].unsqueeze(1).broadcast_to([RR, NQB, QB]),
                            op0=ALU.add, op1=ALU.mult)
                    last.then_inc(qrel_ready.sem, 1)

                def copy_pT(n):
                    dve.wait_ge(pT_ps.sem, pT_ps.at(b, n + 1))
                    t, c = n // QPT, n // QPT + 1
                    if t >= 2:
                        dve.wait_ge(av_ps.sem, av_ps.at(b, t - 1))
                    nc.vector.tensor_copy(
                        probsT[t % 2][:, 0:c, :, (n % QPT) * QB:(n % QPT + 1) * QB],
                        ps[:, 4 + n % 2, 0:c * P].rearrange("p (c h i) -> p c h i", h=H, i=QB)
                    ).then_inc(pT_dve.sem, 1)

                def divide_out(t):
                    dve.wait_ge(av_ps.sem, av_ps.at(b, t + 1))
                    o = ps[:, 6, 0:H * (D + 1)].rearrange("p (h d) -> p h d", d=D + 1)
                    step(nc.vector.reciprocal(den[:, t, :], o[:, :, D]))
                    nc.vector.tensor_tensor(out=attn[:, t, :].rearrange("p (h d) -> p h d", d=D),
                                            in0=o[:, :, 0:D],
                                            in1=den[:, t, :].unsqueeze(2).broadcast_to([P, H, D]),
                                            op=ALU.mult).then_inc(attn_ready.sem, 1)

                for n in range(NQB):
                    dve.wait_ge(scores_ready.sem, scores_ready.at(b, n + 1))
                    if n >= 8:
                        dve.wait_ge(exp_ready.sem, exp_ready.at(b, n - 7))
                    nc.vector.tensor_reduce(neg_max[:, n % 8:n % 8 + 1], ps[:, n % NB, 0:QB * (n + 1)],
                                            axis=AXX, op=ALU.max, negate=True).then_inc(max_ready.sem, 1)
                    if n >= 3 and (n - 3) % 2 == 0:
                        copy_pT(n - 3)
                    if n >= QPT and n % QPT == 5:
                        divide_out(n // QPT - 1)
                copy_pT(NQB - 2)
                divide_out(T - 1)
                dve.wait_ge(y_ready.sem, y_ready.at(b, 1))
                step(norm_out(y_bank, x))

                norm_in(1)
                for f in range(FT):
                    dve.wait_ge(ge_ready.sem, ge_ready.at(b, f + 1))
                    step(nc.vector.tensor_scalar(hid_e[:, f, :], hid_e[:, f, :], 1.0, None, ALU.add))
                    step(nc.vector.reciprocal(hid_e[:, f, :], hid_e[:, f, :]))
                    step(nc.vector.tensor_tensor(out=hid_e[:, f, :], in0=hid_e[:, f, :], in1=ps[:, f, :],
                                                 op=ALU.mult))
                    dve.wait_ge(gu_ps.sem, gu_ps.at(b, 2 * f + 2))
                    nc.vector.tensor_tensor(out=hid[:, f, :], in0=hid_e[:, f, :], in1=ps[:, 3 + f, :],
                                            op=ALU.mult).then_inc(hid_ready.sem, 1)
                dve.wait_ge(y_ready.sem, y_ready.at(b, 2))
                step(norm_out(y_bank, x))

                norm_in(2)
                for w in range(2):
                    dve.wait_ge(qnorm_ready.sem, qnorm_ready.at(b, w + 1))
                    nc.vector.tensor_tensor(out=(qT, kT)[w][:], in0=lin[:, w, :], in1=lin_sq[:, w, :],
                                            op=ALU.mult).then_inc(qk_ready.sem, 1)
                dve.wait_ge(qk_ready.sem, qk_ready.at(b, 2))
                for h in range(H):
                    nc.vector.tensor_scalar(q_wide2[:, h, :], qT[:], head_mask[:, h:h + 1], None,
                                            ALU.mult).then_inc(qwide2_ready.sem, 1)
                dve.wait_ge(av2_ps.sem, av2_ps.at(b, H))
                for a in range(2):
                    o = ps[:, 4 + a, 0:2 * H * (D + 1)].rearrange("p (n d) -> p n d", d=D + 1)
                    dn = den[:, 2 * a:2 * a + 2, :].rearrange("p t h -> p (t h)")
                    step(nc.vector.reciprocal(dn, o[:, :, D]))
                    nc.vector.tensor_tensor(
                        out=attn[:, 2 * a:2 * a + 2, :].rearrange("p t (h d) -> p (t h) d", d=D),
                        in0=o[:, :, 0:D], in1=dn.unsqueeze(2).broadcast_to([P, 2 * H, D]),
                        op=ALU.mult).then_inc(attn_ready.sem, 1)
                dve.wait_ge(y_ready.sem, y_ready.at(b, 3))
                step(norm_out(y_bank, x))

                norm_in(3)
                dve.wait_ge(router_ps.sem, router_ps.at(b, 1))
                lg = ps[:, 6, 0:T * NE].rearrange("p (t e) -> p t e", t=T)

                def per_token(a):
                    return a.broadcast_to([P, T, NE])

                step(nc.vector.tensor_reduce(router_s[:, :, 0], lg, axis=AXX, op=ALU.max, negate=True))
                nc.vector.tensor_tensor(out=router[:], in0=lg, in1=per_token(router_s[:, :, 0:1]), op=ALU.add
                                        ).then_inc(router_in.sem, 1)
                dve.wait_ge(router_exp.sem, router_exp.at(b, 1))
                step(nc.vector.tensor_reduce(router_s[:, :, 1], router_e[:], axis=AXX, op=ALU.add))
                step(nc.vector.reciprocal(router_s[:, :, 0], router_s[:, :, 1]))
                step(nc.vector.tensor_tensor(out=router[:], in0=router_e[:], in1=per_token(router_s[:, :, 0:1]),
                                             op=ALU.mult))
                carry_wait()
                for t in range(T):
                    last = nc.vector.max(top8[:, t, :], router[:, t, :])
                step(last)
                carry_wait()
                for t in range(T):
                    last = nc.vector.max_index(top_idx[:, t, :], top8[:, t, :], router[:, t, :])
                step(last)
                step(nc.vector.tensor_copy(top_idx_f[:], top_idx[:]))
                numbers = expert_no[:].unsqueeze(1).broadcast_to([P, T, NE])
                for j, g in enumerate((gates, gates2)):
                    step(nc.vector.tensor_tensor(out=g[:], in0=numbers, in1=per_token(top_idx_f[:, :, j:j + 1]),
                                                 op=ALU.is_equal))
                    step(nc.vector.tensor_tensor(out=g[:], in0=g[:], in1=per_token(top8[:, :, j:j + 1]),
                                                 op=ALU.mult))
                nc.vector.tensor_tensor(out=gates[:], in0=gates[:], in1=gates2[:], op=ALU.add
                                        ).then_inc(gates_ready.sem, 1)
                dve.wait_ge(accb_ps.sem, accb_ps.at(b, 1))
                step(nc.vector.tensor_copy(acc, y_bank))
                for e in range(NE):
                    dve.wait_ge(moe_y_ps.sem, moe_y_ps.at(b, e + 1))
                    for t in range(T):
                        last = nc.vector.scalar_tensor_tensor(
                            out=acc[:, t, :], in0=ps[:, 4 + e % 2, t * P:(t + 1) * P],
                            scalar=gates[:, t, e:e + 1], in1=acc[:, t, :], op0=ALU.mult, op1=ALU.add)
                    last.then_inc(moe_y_used.sem, 1)
                    dve.wait_ge(moe_y_used.sem, moe_y_used.at(b, e + 1))
                dve.wait_ge(x_stored.sem, x_stored.at(b, 0))
                norm_out(acc, x_out).then_inc(x_final.sem, 1)
                assert count[0] == dve_step.per, count[0]

        @block.tensor
        def _(pe):
            mm = nc.tensor.matmul
            pe.wait_ge(consts_ready, 1)
            waited_moe = False
            for n, (kind, a) in enumerate(groups):
                if n == 0:
                    pe.wait_ge(ld_attn, (9 + 2 * QB) * 16)
                    pe.wait_ge(rep_ready, 3)
                if n == 1:
                    pe.wait_ge(wf_ready, 1)
                if n == first_moe:
                    pe.wait_ge(ld_moe, 5 * 16)
                if n >= PREP_BANKS:
                    ca, cd = copies(n - PREP_BANKS)
                    if ca:
                        pe.wait_ge(prep_act, ca)
                    if cd:
                        pe.wait_ge(prep_dve, cd)
                bank = ps[:, n % PREP_BANKS, :]
                if kind == "rel":
                    for c in range(NREL // P):
                        last = mm(bank[0:RR, c * P:(c + 1) * P],
                                  rel_rep[:, c, :, :], ident[:], start=True, stop=True)
                elif kind in ("gate_up", "down"):
                    for f in range(FT):
                        last = nc.tensor.transpose(bank[:, f * P:(f + 1) * P],
                                                   wf_in[:, a, f * P:(f + 1) * P], ident[:])
                elif kind == "small":
                    nc.tensor.transpose(bank[:, 0:NE], gate_in, ident[0:NE, 0:NE])
                    for m in range(MF):
                        last = nc.tensor.transpose(bank[:, NE * (m + 1):NE * (m + 2)],
                                                   b1_in[:, m * P:(m + 1) * P], ident[0:NE, 0:NE])
                elif kind == "w1":
                    for m in range(MF):
                        last = nc.tensor.transpose(bank[:, m * P:(m + 1) * P], w1_in[:, m, a, :], ident[:])
                else:
                    for m in range(MF):
                        last = nc.tensor.transpose(bank[:, m * P:(m + 1) * P],
                                                   w2_in[:, a, m * P:(m + 1) * P], ident[:])
                last.then_inc(prep_done, 1)
            pe.wait_ge(prep_act, (len(groups) + 1) // 2)
            pe.wait_ge(prep_dve, len(groups) // 2)
            pe.wait_ge(j_ready, 2)
            pe.wait_ge(qb_ready, 8)
            row = qbias_row[:].rearrange("a m c o -> a m (c o)")
            for m in range(2):
                mm(ps[:, 7, 2 + m:3 + m], row[:, m, :], ones[:, 0:1], start=True, stop=True)
            mm(ps[:, 7, 0:1], ones[:], j_sum[:], start=True, stop=True).then_inc(j_ready, 1)
            pe.wait_ge(j_ready, 5)
            pe.wait_ge(toep_dma, 16 * QB)

            with pe.Fori(0, B) as b:
                def input_T(k):
                    for t in range(T):
                        pe.wait_ge(xn_ready.sem, xn_ready.at(b, k * T + t + 1))
                        last = nc.tensor.transpose(ps[:, 6, t * P:(t + 1) * P], xn[:, t, :], ident[:])
                    last.then_inc(xnT_ps.sem, 1)
                    pe.wait_ge(xnT_ready.sem, xnT_ready.at(b, k + 1))

                def token_major(bank, t, w, bias, src):
                    o = ps[:, bank, t * P:(t + 1) * P]
                    mm(o, src[:, t * P:(t + 1) * P], w, start=True, stop=False)
                    return mm(o, ones[:], bias, start=False, stop=True)

                input_T(0)
                mm(ps[:, 0, :], w_qkvo[:, 0, :], xnT[:], start=True, stop=True).then_inc(proj_ps.sem, 1)
                mm(ps[:, 1, :], w_qkvo[:, 1, :], xnT[:], start=True, stop=True).then_inc(proj_ps.sem, 1)
                for t in range(T):
                    last = token_major(2, t, w_qkvo[:, 2, :], bias_rows[:, 0, :], xnT)
                last.then_inc(proj_ps.sem, 1)
                for c in range(H // 2):
                    if c >= 3:
                        pe.wait_ge(qrel_ready.sem, qrel_ready.at(b, c - 2))
                    mm(ps[:, 3 + c % 3, :], wq_rep[:, c, :, :, :], xnT[:], start=True, stop=True
                       ).then_inc(qrel_ps.sem, 1)
                pe.wait_ge(qrel_ready.sem, qrel_ready.at(b, H // 2))
                pe.wait_ge(proj_copied.sem, proj_copied.at(b, 3))

                def scores(n):
                    if n % QPT == 0:
                        pe.wait_ge(qwide_ready.sem, qwide_ready.at(b, n // QPT + 1))
                    if n >= NB:
                        pe.wait_ge(exp_ready.sem, exp_ready.at(b, n - NB + 1))
                    L = QB * (n + 1)
                    o = ps[:, n % NB, 0:L]
                    mm(o, q_wide0[:, n, :, :], kT[:, 0:L], start=True, stop=False)
                    mm(o, q_rel[:, n, :, :], toep[:, S - L:S], start=False, stop=True
                       ).then_inc(scores_ready.sem, 1)

                def transpose_probs(n):
                    pe.wait_ge(exp_ready.sem, exp_ready.at(b, n + 1))
                    if n >= 2:
                        done = (pT_dve, pT_act)[n % 2]
                        pe.wait_ge(done.sem, done.at(b, n // 2))
                    for c in range(n // QPT + 1):
                        last = nc.tensor.transpose(ps[:, 4 + n % 2, c * P:(c + 1) * P],
                                                   probs[:, n % NB, c * P:(c + 1) * P], ident[:])
                    last.then_inc(pT_ps.sem, 1)

                def weigh_values(t):
                    pe.wait_ge(pT_dve.sem, pT_dve.at(b, (t + 1) * QPT // 2))
                    pe.wait_ge(pT_act.sem, pT_act.at(b, (t + 1) * QPT // 2))
                    for h in range(H):
                        for c in range(t + 1):
                            last = mm(ps[:, 6, h * (D + 1):(h + 1) * (D + 1)], probsT[t % 2][:, c, h, :],
                                      v_ones[:, c, h, :], start=(c == 0), stop=(c == t))
                    last.then_inc(av_ps.sem, 1)

                def attn_T(t):
                    pe.wait_ge(attn_ready.sem, attn_ready.at(b, t + 1))
                    nc.tensor.transpose(ps[:, 6, 256:256 + P], attn[:, t, :], ident[:]
                                        ).then_inc(attnT_ps.sem, 1)

                def project(t):
                    pe.wait_ge(attnT_ready.sem, attnT_ready.at(b, t + 1))
                    return token_major(7, t, w_qkvo[:, 3, :], bias_rows[:, 1, :], attnT)

                for n in range(3):
                    scores(n)
                for n in range(NQB):
                    if n + 3 < NQB:
                        scores(n + 3)
                    transpose_probs(n)
                    t = n // QPT - 1
                    if t >= 0 and n % QPT == 3:
                        weigh_values(t)
                    if t >= 0 and n % QPT == 5:
                        attn_T(t)
                    if t >= 0 and n % QPT == 8:
                        project(t)
                weigh_values(T - 1)
                attn_T(T - 1)
                project(T - 1).then_inc(y_ready.sem, 1)

                input_T(1)
                for f in range(FT):
                    mm(ps[:, f, :], wgT[:, f * P:(f + 1) * P], xnT[:], start=True, stop=True
                       ).then_inc(gu_ps.sem, 1)
                    mm(ps[:, 3 + f, :], wuT[:, f * P:(f + 1) * P], xnT[:], start=True, stop=True
                       ).then_inc(gu_ps.sem, 1)
                pe.wait_ge(hid_ready.sem, hid_ready.at(b, FT))
                for t in range(T):
                    for f in range(FT):
                        last = mm(ps[:, 7, t * P:(t + 1) * P], hid[:, f, t * P:(t + 1) * P], wdT[:, f, :],
                                  start=(f == 0), stop=(f == FT - 1))
                last.then_inc(y_ready.sem, 1)

                input_T(2)
                wq2 = w_quat[:].rearrange("p m c o -> p m (c o)")
                for w in range(2):
                    mm(ps[:, w, :], wq2[:, w, :], xnT[:], start=True, stop=True).then_inc(proj_ps.sem, 1)
                for t in range(T):
                    last = token_major(2, t, wq2[:, 2, :], row[:, 2, :], xnT)
                last.then_inc(proj_ps.sem, 1)
                for w in range(2):
                    pe.wait_ge(proj_copied.sem, proj_copied.at(b, 3 + 2 * (w + 1)))
                    mm(ps[:, 3 + w, :], same_part[:], lin_sq[:, w, :], start=True, stop=True
                       ).then_inc(norm_ps.sem, 1)
                pe.wait_ge(proj_copied.sem, proj_copied.at(b, 8))
                pe.wait_ge(qk_ready.sem, qk_ready.at(b, 2))

                def scores2(h):
                    pe.wait_ge(qwide2_ready.sem, qwide2_ready.at(b, h + 1))
                    for a in range(2):
                        if h >= 1:
                            pe.wait_ge(e2_ready.sem, e2_ready.at(b, 2 * h - 1 + a))
                        for c in range(2 * a, 2 * a + 2):
                            last = mm(ps[:, c, :], kT[:, c * P:(c + 1) * P], q_wide2[:, h, :],
                                      start=True, stop=True)
                        last.then_inc(s2_ready.sem, 1)

                scores2(0)
                for h in range(H):
                    if h + 1 < H:
                        scores2(h + 1)
                    pe.wait_ge(e2_ready.sem, e2_ready.at(b, 2 * h + 2))
                    for t in range(T):
                        for c in range(T):
                            at = ((t % 2) * H + h) * (D + 1)
                            last = mm(ps[:, 4 + t // 2, at:at + D + 1],
                                      head_probs[:, h % 2, c, t * P:(t + 1) * P],
                                      v_ones[:, c, h, :], start=(c == 0), stop=(c == T - 1))
                    last.then_inc(av2_ps.sem, 1)
                for t in range(T):
                    pe.wait_ge(attn_ready.sem, attn_ready.at(b, T + t // 2 + 1))
                    last = nc.tensor.transpose(ps[:, 6, t * P:(t + 1) * P], attn[:, t, :], ident[:])
                last.then_inc(attnT_ps.sem, 1)
                pe.wait_ge(attnT_ready.sem, attnT_ready.at(b, T + 1))
                for t in range(T):
                    last = token_major(7, t, wq2[:, 3, :], row[:, 3, :], attnT)
                last.then_inc(y_ready.sem, 1)

                input_T(3)
                for t in range(T):
                    last = mm(ps[:, 6, t * NE:(t + 1) * NE], xnT[:, t * P:(t + 1) * P], gateT[:],
                              start=True, stop=True)
                last.then_inc(router_ps.sem, 1)

                def expert_up(e):
                    for m in range(MF):
                        n = e * MF + m
                        if n >= NB:
                            pe.wait_ge(moe_h_ready.sem, moe_h_ready.at(b, n - NB + 1))
                        mm(ps[:, n % NB, :], w1T[:, e, m * P:(m + 1) * P], xnT[:], start=True, stop=True
                           ).then_inc(moe_h_ps.sem, 1)

                def expert_down(e):
                    pe.wait_ge(moe_h_ready.sem, moe_h_ready.at(b, (e + 1) * MF))
                    if e >= 2:
                        pe.wait_ge(moe_y_used.sem, moe_y_used.at(b, e - 1))
                    for t in range(T):
                        for m in range(MF):
                            last = mm(ps[:, 4 + e % 2, t * P:(t + 1) * P],
                                      moe_h[:, e % 2, m, t * P:(t + 1) * P], w2T[:, m, e, :],
                                      start=(m == 0), stop=(m == MF - 1))
                    last.then_inc(moe_y_ps.sem, 1)

                expert_up(0)
                pe.wait_ge(gates_ready.sem, gates_ready.at(b, 1))
                for t in range(T):
                    last = nc.tensor.transpose(ps[0:NE, 7, t * P:(t + 1) * P], gates[:, t, :], ident[:])
                last.then_inc(gatesT_ps.sem, 1)
                pe.wait_ge(gatesT_ready.sem, gatesT_ready.at(b, 1))
                for t in range(T):
                    last = mm(ps[:, 7, t * P:(t + 1) * P], gates_T[:, t, :], b2_sb[:], start=True, stop=True)
                last.then_inc(accb_ps.sem, 1)
                for e in range(NE):
                    if e + 1 < NE:
                        expert_up(e + 1)
                    expert_down(e)


_INS = ['L0_attn_x', 'L0_attn_Wq', 'L0_attn_bq', 'L0_attn_Wk', 'L0_attn_bk', 'L0_attn_Wv', 'L0_attn_bv',
        'L0_attn_Wo', 'L0_attn_bo', 'L0_attn_rel_key', 'L0_ffn_w_gate', 'L0_ffn_w_up', 'L0_ffn_w_down',
        'L1_attn_qW', 'L1_attn_qb', 'L1_attn_kW', 'L1_attn_kb', 'L1_attn_vW', 'L1_attn_vb', 'L1_attn_oW',
        'L1_attn_ob', 'L1_attn_J', 'L1_ffn_gate_w', 'L1_ffn_w1', 'L1_ffn_b1', 'L1_ffn_w2', 'L1_ffn_b2']


def kernel(**inputs):
    import numpy as _np
    import concourse.bacc as _bacc
    from concourse import mybir as _mybir
    from concourse.bass_utils import run_bass_kernel_spmd as _run

    nc = _bacc.Bacc("TRN2", target_bir_lowering=False, num_devices=1)
    arrays, args = {}, []
    for name in _INS:
        a = _np.ascontiguousarray(inputs[name])
        arrays[f"in_{name}_dram"] = a
        args.append(nc.dram_tensor(f"in_{name}_dram", a.shape, _mybir.dt.from_np(a.dtype), kind="ExternalInput").ap())
    shape = _np.shape(inputs['L0_attn_x'])
    o = nc.dram_tensor("out_dram", shape, _mybir.dt.float32, kind="ExternalOutput").ap()
    build_sandwich(nc, *args, o)
    r = _run(nc, [arrays], core_ids=[0])
    return r.results[0]["out_dram"]
```

```python
import numpy as np
import concourse.bass as bass
from concourse import mybir
from contextlib import ExitStack


class Signal:

    def __init__(self, sem, per, base=0):
        self.sem, self.per, self.base = sem, per, base

    def at(self, batch, n):
        return batch * self.per + (self.base + n)


def build_sandwich(nc, X, Wq, bq, Wk, bk, Wv, bv, Wo, bo, rel_key, w_gate, w_up, w_down,
                   qW, qb, kW, kb, vW, vb, oW, ob, J, gate_w, w1, b1, w2, b2, out):
    f32, f32r, i32, u32 = mybir.dt.float32, mybir.dt.float32r, mybir.dt.int32, mybir.dt.uint32
    ALU = mybir.AluOpType
    ACT = mybir.ActivationFunctionType
    AXX = mybir.AxisListType.X

    B, S, E = X.shape
    P = 128
    T = S // P
    NREL, D = rel_key.shape
    H = E // D
    QB = P // H
    NQB = S // QB
    QPT = P // QB
    RR = QB * D
    HID = w_gate.shape[0]
    FT = HID // P
    NF, NE, _ = w1.shape
    MF = NF // P
    GH = 4
    HG = H // GH
    GR = GH * D
    QD = E // 4
    SCALE = float(D) ** -0.5
    DEQ = 1.0 / 127.0
    LN_EPS, QN_EPS = 1e-5, 1e-6
    MASKED = -1e30
    TWO_PI = 2.0 * np.pi
    NB = 4

    ctx = ExitStack()
    with ctx:
        nc.disable_value_cache = True

        def sb(name, shape, dt=f32):
            return ctx.enter_context(nc.sbuf_tensor(name, shape, dt))

        def sem(name):
            return ctx.enter_context(nc.semaphore(name))

        ident = sb("ident", [P, P])
        ones = sb("ones", [1, P])
        group_mask = sb("group_mask", [P, GH])
        head_mask = sb("head_mask", [P, H])
        query_mask = sb("query_mask", [P, QB])
        same_part = sb("same_part", [P, P])
        signs = sb("signs", [P, 4])
        eps_col = sb("eps_col", [P, 1])
        spare = sb("spare", [P, 4])
        expert_no = sb("expert_no", [P, NE])
        toep = sb("toep", [RR + QB, S])
        rel_rows = sb("rel_rows", [RR, NREL])
        w_qkvo = sb("w_qkvo", [P, 4, P])
        q_bias = sb("q_bias", [P, 1])
        k_bias = sb("k_bias", [P, 1])
        wq_rep = sb("wq_rep", [P, H // 2, 2, QB, D])
        q_bias_rep = sb("q_bias_rep", [P, H // 2])
        bias_rows = sb("bias_rows", [1, 2, P])
        rel_in = sb("rel_in", [P, NREL // P, D])
        wgT = sb("wgT", [P, HID])
        wuT = sb("wuT", [P, HID])
        wdT = sb("wdT", [P, FT, P])
        w_quat = sb("w_quat", [P, 4, 4, QD])
        qbias_in = sb("qbias_in", [1, 4, 4, QD])
        qbias_row = sb("qbias_row", [1, 4, 4, QD])
        qbias_col = sb("qbias_col", [P, 2])
        j_row = sb("j_row", [1, P])
        j_turn = sb("j_turn", [1, P])
        j_sum = sb("j_sum", [1, 1])
        j_bias = sb("j_bias", [P, 1])
        w1T = sb("w1T", [P, NE, NF])
        w2T = sb("w2T", [P, MF, NE, P])
        gateT = sb("gateT", [P, NE])
        b1T = sb("b1T", [P, MF, NE])
        b2_sb = sb("b2_sb", [NE, P])
        x_in = sb("x_in", [P, T, E])
        x = sb("x", [P, T, E])
        x_out = sb("x_out", [P, T, E])
        stats = sb("stats", [P, T, 6])
        moments = sb("moments", [P, T, 2])
        rstd = sb("rstd", [P, T])
        root = sb("root", [P, 3, T])
        xn = sb("xn", [P, T, E])
        xnT = sb("xnT", [P, S])
        qT = sb("qT", [P, S])
        kT = sb("kT", [P, S])
        v_ones = sb("v_ones", [P, T, H, D + 1])
        with ExitStack() as shared:
            k_parts = shared.enter_context(nc.sbuf_tensor("k_parts", [P, HG, S], f32r))
            q_parts = shared.enter_context(nc.sbuf_tensor("q_parts", [P, HG, S], f32r))
            q_heads = shared.enter_context(nc.sbuf_tensor("q_heads", [P, 2, GH, S], f32r))
        q_wide = sb("q_wide", [P, NQB * H * QB])
        halves = q_heads[:, 1, :, :]
        q_rel = sb("q_rel", [RR + QB, NQB, H, QB])
        probs = sb("probs", [P, NB, S])
        pT_all = sb("pT_all", [P, (2 * T - 1) * H * P])
        neg_max = sb("neg_max", [P, 8])
        den = sb("den", [P, T, H])
        attn = xn
        attnT = xnT
        q_wide0 = q_wide[:].rearrange("p (n h i) -> p n h i", h=H, i=QB)
        pT_flat = pT_all[:]
        pT_odd = (T - 1) * H * P
        probsT = [pT_flat[:, 0:pT_odd].rearrange("p (c h i) -> p c h i", c=T - 1, h=H),
                  pT_flat[:, pT_odd:].rearrange("p (c h i) -> p c h i", c=T, h=H)]
        w1_in = pT_flat[:, 0:MF * NE * P].rearrange("p (m e d) -> p m e d", m=MF, e=NE)
        w2_in = pT_flat[:, MF * NE * P:2 * MF * NE * P].rearrange("p (e f) -> p e f", e=NE)
        o0 = 2 * MF * NE * P
        wi_in = pT_flat[:, o0:o0 + 3 * HID].bitcast(i32).rearrange("p (w n) -> p w n", w=3)
        wf_in = pT_flat[:, o0 + 3 * HID:o0 + 6 * HID].rearrange("p (w n) -> p w n", w=3)
        b1_in = pT_flat[0:NE, o0 + 6 * HID:o0 + 6 * HID + NF]
        gate_in = pT_flat[0:NE, o0 + 6 * HID + NF:o0 + 6 * HID + NF + P]
        rel_rep = pT_flat[:, o0 + 6 * HID + NF + P:o0 + 6 * HID + NF + P + RR * NREL // P].rearrange(
            "p (a i d) -> p a i d", a=NREL // P, i=QB)
        hp = 2 * GH * 2 * S
        head_probs = pT_flat[:, 0:hp].rearrange("p (a g c s) -> p a g c s", a=2, g=GH, c=2)
        lin = pT_flat[:, hp:hp + 2 * S].rearrange("p (w s) -> p w s", w=2)
        lin_sq = pT_flat[:, hp + 2 * S:hp + 4 * S].rearrange("p (w s) -> p w s", w=2)
        outT = qT
        hid_e = pT_flat[:, 0:FT * S].rearrange("p (f s) -> p f s", f=FT)
        hid = pT_flat[:, FT * S:2 * FT * S].rearrange("p (f s) -> p f s", f=FT)
        moe_h = pT_flat[:, 0:2 * MF * S].rearrange("p (a f s) -> p a f s", a=2, f=MF)
        acc = pT_flat[:, 2 * MF * S:2 * MF * S + T * E].rearrange("p (t d) -> p t d", t=T)
        router = sb("router", [P, T, NE])
        router_e = sb("router_e", [P, T, NE])
        router_s = sb("router_s", [P, T, 2])
        top8 = sb("top8", [P, T, 8])
        top_idx = sb("top_idx", [P, T, 8], u32)
        top_idx_f = sb("top_idx_f", [P, T, 8])
        gates = sb("gates", [P, T, NE])
        gates2 = sb("gates2", [P, T, NE])
        gates_T = sb("gates_T", [NE, T, P])

        ps = ctx.enter_context(nc.psum_tensor("ps", [P, 8, 512], f32))

        ld_attn, ld_ffn, ld_quat, ld_moe = sem("ld_attn"), sem("ld_ffn"), sem("ld_quat"), sem("ld_moe")
        toep_dma = sem("toep_dma")
        pool_step = sem("pool_step")
        consts_ready = sem("consts_ready")
        prep_done = sem("prep_done")
        prep_act = sem("prep_act")
        prep_dve = sem("prep_dve")
        rep_ready = sem("rep_ready")
        wf_ready = sem("wf_ready")
        prep_chain = sem("prep_chain")
        j_ready = sem("j_ready")
        toep_base = sem("toep_base")
        qb_ready = sem("qb_ready")
        x_loaded = Signal(sem("x_loaded"), 16)
        x_copied = Signal(sem("x_copied"), 1, base=1)
        x_final = Signal(sem("x_final"), 1, base=1)
        x_stored = Signal(sem("x_stored"), 16, base=16)
        dve_step = Signal(sem("dve_step"), 152)
        xn_ready = Signal(sem("xn_ready"), 4 * T)
        xnT_ps = Signal(sem("xnT_ps"), 4)
        xnT_ready = Signal(sem("xnT_ready"), 4)
        y_ready = Signal(sem("y_ready"), 3)
        proj_ps = Signal(sem("proj_ps"), 6)
        proj_copied = Signal(sem("proj_copied"), 8)
        qrel_ps = Signal(sem("qrel_ps"), H // 2)
        qrel_ready = Signal(sem("qrel_ready"), H // 2)
        qwide_ready = Signal(sem("qwide_ready"), T)
        probs_zero = Signal(sem("probs_zero"), 1)
        scores_ready = Signal(sem("scores_ready"), NQB)
        max_ready = Signal(sem("max_ready"), NQB)
        exp_ready = Signal(sem("exp_ready"), NQB)
        pT_ps = Signal(sem("pT_ps"), NQB)
        pT_dve = Signal(sem("pT_dve"), NQB // 2)
        pT_act = Signal(sem("pT_act"), NQB // 2)
        av_ps = Signal(sem("av_ps"), T)
        outT_ready = Signal(sem("outT_ready"), T + HG)
        turned_ps = Signal(sem("turned_ps"), T + HG)
        attn_ready = Signal(sem("attn_ready"), T + HG)
        attnT_ps = Signal(sem("attnT_ps"), T + 1)
        attnT_ready = Signal(sem("attnT_ready"), T + 1)
        gu_ps = Signal(sem("gu_ps"), 2 * FT)
        ge_ready = Signal(sem("ge_ready"), FT)
        hid_ready = Signal(sem("hid_ready"), FT)
        norm_ps = Signal(sem("norm_ps"), 2)
        qnorm_ready = Signal(sem("qnorm_ready"), 2)
        act_step = Signal(sem("act_step"), 2)
        qk_ready = Signal(sem("qk_ready"), 2)
        parts_ready = Signal(sem("parts_ready"), HG)
        q_heads_ready = Signal(sem("q_heads_ready"), H)
        s2_ready = Signal(sem("s2_ready"), 2 * H)
        e2_ready = Signal(sem("e2_ready"), 2 * H)
        av2_ps = Signal(sem("av2_ps"), 2 * HG)
        router_ps = Signal(sem("router_ps"), 1)
        router_in = Signal(sem("router_in"), 1)
        router_exp = Signal(sem("router_exp"), 1)
        gates_ready = Signal(sem("gates_ready"), 1)
        gatesT_ps = Signal(sem("gatesT_ps"), 1)
        gatesT_ready = Signal(sem("gatesT_ready"), 1)
        accb_ps = Signal(sem("accb_ps"), 1)
        moe_h_ps = Signal(sem("moe_h_ps"), NE * MF)
        moe_h_ready = Signal(sem("moe_h_ready"), NE * MF)
        moe_y_ps = Signal(sem("moe_y_ps"), NE)
        moe_y_used = Signal(sem("moe_y_used"), NE)

        MATS = [qW, kW, vW, oW]
        QBIAS = [qb, kb, vb, ob]
        PREP_BANKS = 8

        block = ctx.enter_context(nc.Block())

        @block.sync
        def _(sp):
            n = 0
            for j, w in enumerate((Wq, Wk, Wv, Wo)):
                sp.dma_start(w_qkvo[:, j, :], w).then_inc(ld_attn, 16)
            sp.dma_start(q_bias[:], bq.rearrange("(p a) -> p a", a=1)).then_inc(ld_attn, 16)
            sp.dma_start(k_bias[:], bk.rearrange("(p a) -> p a", a=1)).then_inc(ld_attn, 16)
            sp.dma_start(bias_rows[:, 0, :], bv.rearrange("(a p) -> a p", a=1)).then_inc(ld_attn, 16)
            sp.dma_start(bias_rows[:, 1, :], bo.rearrange("(a p) -> a p", a=1)).then_inc(ld_attn, 16)
            sp.dma_start(rel_in[:], rel_key.rearrange("(a p) d -> p a d", p=P)).then_inc(ld_attn, 16)
            for hh in range(2):
                for i in range(QB):
                    r = hh * RR + i * D
                    sp.dma_start(q_bias_rep[r:r + D, :],
                                 bq.rearrange("(c z d) -> z d c", z=2, d=D)[hh],
                                 allow_slow_non_contiguous=True).then_inc(ld_attn, 16)
            sp.dma_start(wi_in[:, 0, :].rearrange("p (f d) -> p f d", f=FT),
                         w_gate.rearrange("(f p) d -> p f d", p=P)).then_inc(ld_ffn, 16)
            sp.dma_start(wi_in[:, 1, :].rearrange("p (f d) -> p f d", f=FT),
                         w_up.rearrange("(f p) d -> p f d", p=P)).then_inc(ld_ffn, 16)
            sp.dma_start(wi_in[:, 2, :], w_down).then_inc(ld_ffn, 16)
            sp.dma_start(w1_in, w1.rearrange("(m p) e d -> p m e d", p=P)).then_inc(ld_moe, 16)
            sp.dma_start(w2_in, w2).then_inc(ld_moe, 16)
            sp.wait_ge(toep_base, 2)
            for i in range(QB):
                c = S - QB - NREL + 1 + i
                sp.dma_start(toep[i * D:(i + 1) * D, c:c + NREL],
                             rel_rows[i * D:(i + 1) * D, :]).then_inc(toep_dma, 16)
            with sp.Fori(0, B) as b:
                sp.wait_ge(x_copied.sem, x_copied.at(b, 0))
                sp.dma_start(x_in[:], X[bass.ds(b, 1)].rearrange("a (t p) e -> p (a t) e", p=P)
                             ).then_inc(x_loaded.sem, 16)
            sp.wait_ge(x_stored.sem, 16 * (B + 1))

        @block.gpsimd
        def _(pool):
            done = [0]

            def step(ins):
                done[0] += 1
                ins.then_inc(pool_step, 1)
                pool.wait_ge(pool_step, done[0])

            step(pool.memset(ident[:], 0.0))
            step(pool.affine_select(out=ident[:], in_=ident[:], compare_op=ALU.not_equal, fill=1.0,
                                    base=0, pattern=[[-1, P]], channel_multiplier=1))
            step(pool.memset(ones[:], 1.0))
            step(pool.memset(eps_col[:], QN_EPS))
            step(pool.memset(head_mask[:], SCALE))
            step(pool.affine_select(out=head_mask[:], in_=head_mask[:], compare_op=ALU.is_ge, fill=0.0,
                                    base=0, pattern=[[-D, H]], channel_multiplier=1))
            step(pool.affine_select(out=head_mask[:], in_=head_mask[:], compare_op=ALU.is_ge, fill=0.0,
                                    base=D - 1, pattern=[[D, H]], channel_multiplier=-1))
            step(pool.memset(group_mask[:], SCALE))
            for r in range(0, P, GR):
                m = group_mask[r:r + GR, :]
                step(pool.affine_select(out=m, in_=m, compare_op=ALU.is_ge, fill=0.0,
                                        base=0, pattern=[[-D, GH]], channel_multiplier=1))
                step(pool.affine_select(out=m, in_=m, compare_op=ALU.is_ge, fill=0.0,
                                        base=D - 1, pattern=[[D, GH]], channel_multiplier=-1))
            step(pool.memset(query_mask[:], SCALE))
            for r in (0, RR):
                m = query_mask[r:r + RR, :]
                step(pool.affine_select(out=m, in_=m, compare_op=ALU.is_ge, fill=0.0,
                                        base=0, pattern=[[-D, QB]], channel_multiplier=1))
                step(pool.affine_select(out=m, in_=m, compare_op=ALU.is_ge, fill=0.0,
                                        base=D - 1, pattern=[[D, QB]], channel_multiplier=-1))
            step(pool.memset(same_part[:], 0.0))
            for k in range(-3, 4):
                step(pool.affine_select(out=same_part[:], in_=same_part[:], compare_op=ALU.not_equal, fill=1.0,
                                        base=k * QD, pattern=[[-1, P]], channel_multiplier=1))
            step(pool.memset(signs[:], 1.0))
            for c, part in ((1, 0), (2, 0), (3, 0), (2, 1), (3, 2), (1, 3)):
                step(pool.memset(signs[c * QD:(c + 1) * QD, part:part + 1], -1.0))
            step(pool.iota(expert_no[:], [[1, NE]], base=0, channel_multiplier=0,
                           allow_small_or_imprecise_dtypes=True))
            step(pool.memset(v_ones[:], 1.0))
            step(pool.memset(toep[RR:RR + QB, :], 0.0))
            step(pool.affine_select(out=toep[RR:RR + QB, :], in_=toep[RR:RR + QB, :], compare_op=ALU.is_ge,
                                    fill=MASKED, base=S - QB, pattern=[[-1, S]], channel_multiplier=1))
            rows = q_rel[RR:RR + QB, :, :, :].rearrange("p n h i -> p (n h) i")
            step(pool.memset(rows, 0.0))
            pool.affine_select(out=rows, in_=rows, compare_op=ALU.not_equal, fill=1.0, base=0,
                               pattern=[[0, NQB * H], [-1, QB]], channel_multiplier=1
                               ).then_inc(consts_ready, 1)

            with pool.Fori(0, B) as b:
                pool.wait_ge(proj_copied.sem, proj_copied.at(b, 1))
                for t in range(T):
                    if t == 1:
                        pool.memset(probs[:], 0.0).then_inc(probs_zero.sem, 1)
                    blocks = slice(t * QPT, (t + 1) * QPT)
                    q_in = qT[:, t * P:(t + 1) * P].rearrange("p (n i) -> p n i", i=QB)
                    pool.tensor_tensor(
                        out=q_wide0[:, blocks, :, :],
                        in0=q_in.unsqueeze(2).broadcast_to([P, QPT, H, QB]),
                        in1=head_mask[:].unsqueeze(1).unsqueeze(3).broadcast_to([P, QPT, H, QB]),
                        op=ALU.mult).then_inc(qwide_ready.sem, 1)

        def prep_groups():
            yield ("rel", None)
            yield ("gate_up", 0)
            yield ("gate_up", 1)
            yield ("down", 2)
            yield ("small", None)
            for e in range(NE):
                yield ("w1", e)
                yield ("w2", e)
        groups = list(prep_groups())
        first_moe = 4

        def prep_copy(eng, copy, which):
            for n, (kind, a) in enumerate(groups):
                if n % 2 != which:
                    continue
                eng.wait_ge(prep_done, n + 1)
                bank = ps[:, n % PREP_BANKS, :]
                if kind == "rel":
                    last = copy(rel_rows[:], bank[0:RR, 0:NREL])
                elif kind == "gate_up":
                    last = copy((wgT, wuT)[a][:], bank[:, 0:HID])
                elif kind == "down":
                    last = copy(wdT[:], bank[:, 0:FT * P].rearrange("p (f d) -> p f d", f=FT))
                elif kind == "small":
                    copy(gateT[:], bank[:, 0:NE])
                    last = copy(b1T[:], bank[:, NE:NE + MF * NE].rearrange("p (m e) -> p m e", m=MF))
                elif kind == "w1":
                    last = copy(w1T[:, a, :], bank[:, :])
                else:
                    last = copy(w2T[:, :, a, :], bank[:, :].rearrange("p (m d) -> p m d", m=MF))
                last.then_inc((prep_act, prep_dve)[which], 1)

        def copies(n):
            return (n // 2 + 1, 0) if n % 2 == 0 else (0, n // 2 + 1)

        @block.scalar
        def _(act):
            for m, w in enumerate(MATS):
                for c in range(4):
                    for part in range(4):
                        act.dma_start(w_quat[c * QD:(c + 1) * QD, m, part, :], w[c ^ part]
                                      ).then_inc(ld_quat, 16)
            for m, w in enumerate(QBIAS):
                act.dma_start(qbias_in[:, m, :, :], w.rearrange("(a w) o -> a w o", a=1)).then_inc(ld_quat, 16)
            act.dma_start(j_row[:], J.rearrange("(a p) -> a p", a=1)).then_inc(ld_quat, 16)
            act.dma_start(gate_in, gate_w).then_inc(ld_moe, 16)
            act.dma_start(b1_in, b1).then_inc(ld_moe, 16)
            act.dma_start(b2_sb[:], b2).then_inc(ld_moe, 16)

            prep_copy(act, lambda o, i: nc.scalar.activation(o, i, ACT.Copy), 0)
            act.wait_ge(consts_ready, 1)
            act.wait_ge(j_ready, 1)
            nc.scalar.activation(j_turn[:], j_row[:], ACT.Sin, accum_out=j_sum[:]).then_inc(j_ready, 1)
            act.wait_ge(j_ready, 3)
            nc.scalar.mul(j_bias[:], ps[:, 7, 0:1], 0.1 / E).then_inc(j_ready, 1)
            nc.scalar.activation(qbias_col[:], ps[:, 7, 2:4], ACT.Copy).then_inc(j_ready, 1)

            with act.Fori(0, B) as b:
                def transposed(k):
                    act.wait_ge(xnT_ps.sem, xnT_ps.at(b, k + 1))
                    nc.scalar.activation(xnT[:], ps[:, 6, :], ACT.Copy).then_inc(xnT_ready.sem, 1)

                transposed(0)
                act.wait_ge(proj_ps.sem, proj_ps.at(b, 1))
                nc.scalar.activation(qT[:], ps[:, 0, :], ACT.Identity, bias=q_bias[:]
                                     ).then_inc(proj_copied.sem, 1)
                act.wait_ge(proj_ps.sem, proj_ps.at(b, 2))
                nc.scalar.activation(kT[:], ps[:, 1, :], ACT.Identity, bias=k_bias[:]
                                     ).then_inc(proj_copied.sem, 1)
                act.wait_ge(proj_ps.sem, proj_ps.at(b, 3))
                nc.scalar.activation(v_ones[:, :, :, 0:D],
                                     ps[:, 2, :].rearrange("p (t h d) -> p t h d", t=T, d=D),
                                     ACT.Copy).then_inc(proj_copied.sem, 1)
                act.wait_ge(probs_zero.sem, probs_zero.at(b, 1))

                def copy_pT(n):
                    act.wait_ge(pT_ps.sem, pT_ps.at(b, n + 1))
                    t, c = n // QPT, n // QPT + 1
                    if t >= 2:
                        act.wait_ge(av_ps.sem, av_ps.at(b, t - 1))
                    nc.scalar.activation(
                        probsT[t % 2][:, 0:c, :, (n % QPT) * QB:(n % QPT + 1) * QB],
                        ps[:, 4 + n % 2, 0:c * P].rearrange("p (c h i) -> p c h i", h=H, i=QB),
                        ACT.Copy).then_inc(pT_act.sem, 1)

                def copy_attnT(t):
                    act.wait_ge(attnT_ps.sem, attnT_ps.at(b, t + 1))
                    nc.scalar.activation(attnT[:, t * P:(t + 1) * P], ps[:, 6, 256:256 + P], ACT.Copy
                                         ).then_inc(attnT_ready.sem, 1)

                for n in range(NQB):
                    act.wait_ge(max_ready.sem, max_ready.at(b, n + 1))
                    if n >= NB:
                        act.wait_ge(pT_ps.sem, pT_ps.at(b, n - NB + 1))
                    L = QB * (n + 1)
                    nc.scalar.activation(probs[:, n % NB, 0:L], ps[:, n % NB, 0:L], ACT.Exp,
                                         bias=neg_max[:, n % 8:n % 8 + 1]).then_inc(exp_ready.sem, 1)
                    if n >= 2 and (n - 2) % 2:
                        copy_pT(n - 2)
                    if n >= QPT and n % QPT == 9:
                        copy_attnT(n // QPT - 1)
                copy_pT(NQB - 1)
                copy_attnT(T - 1)

                transposed(1)
                for f in range(FT):
                    act.wait_ge(gu_ps.sem, gu_ps.at(b, 2 * f + 1))
                    nc.scalar.activation(hid_e[:, f, :], ps[:, f, :], ACT.Exp, scale=-1.0
                                         ).then_inc(ge_ready.sem, 1)

                transposed(2)
                for w in range(2):
                    act.wait_ge(proj_ps.sem, proj_ps.at(b, 3 + w + 1))
                    nc.scalar.activation(lin[:, w, :], ps[:, w, :], ACT.Identity,
                                         bias=qbias_col[:, w:w + 1]).then_inc(proj_copied.sem, 1)
                    nc.scalar.activation(lin_sq[:, w, :], ps[:, w, :], ACT.Square,
                                         bias=qbias_col[:, w:w + 1]).then_inc(proj_copied.sem, 1)
                act.wait_ge(proj_ps.sem, proj_ps.at(b, 6))
                nc.scalar.activation(v_ones[:, :, :, 0:D],
                                     ps[:, 2, :].rearrange("p (t h d) -> p t h d", t=T, d=D),
                                     ACT.Copy).then_inc(proj_copied.sem, 1)
                for w in range(2):
                    act.wait_ge(norm_ps.sem, norm_ps.at(b, w + 1))
                    nc.scalar.activation(lin_sq[:, w, :], ps[:, 3 + w, :], ACT.Ln, bias=eps_col[:]
                                         ).then_inc(act_step.sem, 1)
                for w in range(2):
                    act.wait_ge(act_step.sem, act_step.at(b, w + 1))
                    nc.scalar.activation(lin_sq[:, w, :], lin_sq[:, w, :], ACT.Exp, scale=-0.5
                                         ).then_inc(qnorm_ready.sem, 1)
                for n in range(2 * HG):
                    for g in range(GH):
                        i = n * GH + g
                        act.wait_ge(s2_ready.sem, s2_ready.at(b, i + 1))
                        if n >= 2 and g == 0:
                            act.wait_ge(av2_ps.sem, av2_ps.at(b, n - 1))
                        nc.scalar.activation(head_probs[:, n % 2, g, :, :],
                                             ps[:, 2 * (i % 2):2 * (i % 2) + 2, :], ACT.Exp, bias=j_bias[:]
                                             ).then_inc(e2_ready.sem, 1)
                act.wait_ge(attnT_ps.sem, attnT_ps.at(b, T + 1))
                nc.scalar.activation(attnT[:], ps[:, 6, :], ACT.Copy).then_inc(attnT_ready.sem, 1)

                transposed(3)
                act.wait_ge(router_in.sem, router_in.at(b, 1))
                nc.scalar.activation(router_e[:], router[:], ACT.Exp).then_inc(router_exp.sem, 1)
                act.wait_ge(gatesT_ps.sem, gatesT_ps.at(b, 1))
                nc.scalar.activation(gates_T[:], ps[0:NE, 7, :].rearrange("p (t s) -> p t s", t=T), ACT.Copy
                                     ).then_inc(gatesT_ready.sem, 1)
                for e in range(NE):
                    for m in range(MF):
                        n = e * MF + m
                        act.wait_ge(moe_h_ps.sem, moe_h_ps.at(b, n + 1))
                        if e >= 2 and m == 0:
                            act.wait_ge(moe_y_ps.sem, moe_y_ps.at(b, e - 1))
                        nc.scalar.activation(moe_h[:, e % 2, m, :], ps[:, n % NB, :], ACT.Gelu_apprx_tanh,
                                             bias=b1T[:, m, e:e + 1]).then_inc(moe_h_ready.sem, 1)
                act.wait_ge(x_final.sem, x_final.at(b, 1))
                act.dma_start(out[bass.ds(b, 1)].rearrange("a (t p) e -> p (a t) e", p=P), x_out[:]
                              ).then_inc(x_stored.sem, 16)

        @block.vector
        def _(dve):
            chain = [0]

            def prep(ins):
                chain[0] += 1
                ins.then_inc(prep_chain, 1)
                dve.wait_ge(prep_chain, chain[0])

            dve.wait_ge(ld_attn, (9 + 2 * QB) * 16)
            nc.vector.tensor_copy(rel_rep, rel_in[:].unsqueeze(2).broadcast_to([P, NREL // P, QB, D])
                                  ).then_inc(rep_ready, 1)
            for z in range(2):
                nc.vector.tensor_copy(wq_rep[:, :, z, :, :],
                                      w_qkvo[:, 0, :].rearrange("p (c z d) -> p c z d", z=2, d=D)[:, :, z, :]
                                      .unsqueeze(2).broadcast_to([P, H // 2, QB, D])).then_inc(rep_ready, 1)
            dve.wait_ge(ld_ffn, 3 * 16)
            nc.vector.tensor_scalar(wf_in, wi_in, DEQ, None, ALU.mult).then_inc(wf_ready, 1)
            prep_copy(dve, lambda o, i: nc.vector.tensor_copy(o, i), 1)
            dve.wait_ge(prep_act, 1)
            nc.vector.tensor_copy(toep[0:RR, 0:NREL], rel_rows[:, 0:1].broadcast_to([RR, NREL])
                                  ).then_inc(toep_base, 1)
            nc.vector.tensor_copy(toep[0:RR, NREL:S], rel_rows[:, NREL - 1:NREL].broadcast_to([RR, S - NREL])
                                  ).then_inc(toep_base, 1)
            dve.wait_ge(ld_quat, (4 * 16 + 5) * 16)
            dve.wait_ge(consts_ready, 1)
            wq_all = w_quat[:].rearrange("p m c o -> p m (c o)")
            for m in range(4):
                nc.vector.tensor_tensor(out=w_quat[:, m, :, :], in0=w_quat[:, m, :, :],
                                        in1=signs[:].unsqueeze(2).broadcast_to([P, 4, QD]),
                                        op=ALU.mult).then_inc(qb_ready, 1)
            SIGN = {0: "+---", 1: "+++-", 2: "+-++", 3: "++-+"}
            for w in range(1, 4):
                for part in range(4):
                    src = qbias_in[:, :, 0, :] if w == 1 else qbias_row[:, :, part, :]
                    ins = nc.vector.tensor_tensor(out=qbias_row[:, :, part, :], in0=src,
                                                  in1=qbias_in[:, :, w, :],
                                                  op=ALU.add if SIGN[part][w] == "+" else ALU.subtract)
                    if w < 3:
                        prep(ins)
                    else:
                        ins.then_inc(qb_ready, 1)
            BIG = 1.5 * 2.0 ** 23
            c1 = 6.28125
            c2 = float(np.float32(TWO_PI - c1))
            prep(nc.vector.tensor_scalar(j_turn[:], j_row[:], 1.0 / TWO_PI, BIG, ALU.mult, ALU.add))
            prep(nc.vector.tensor_scalar(j_turn[:], j_turn[:], BIG, None, ALU.subtract))
            prep(nc.vector.scalar_tensor_tensor(out=j_row[:], in0=j_turn[:], scalar=-c1, in1=j_row[:],
                                                op0=ALU.mult, op1=ALU.add))
            prep(nc.vector.scalar_tensor_tensor(out=j_row[:], in0=j_turn[:], scalar=-c2, in1=j_row[:],
                                                op0=ALU.mult, op1=ALU.add))
            PI_IN = float(np.nextafter(np.float32(np.pi), np.float32(0)))
            nc.vector.tensor_scalar(j_row[:], j_row[:], PI_IN, -PI_IN, ALU.min, ALU.max).then_inc(j_ready, 1)
            dve.wait_ge(j_ready, 5)
            nc.vector.memset(spare[:, 1:2], 0.0).then_inc(x_copied.sem, 1)
            nc.vector.memset(spare[:, 2:3], 0.0).then_inc(x_final.sem, 1)
            nc.vector.memset(spare[:, 3:4], 0.0).then_inc(x_stored.sem, 16)

            with dve.Fori(0, B) as b:
                count = [0]

                def step(ins):
                    count[0] += 1
                    ins.then_inc(dve_step.sem, 1)
                    dve.wait_ge(dve_step.sem, dve_step.at(b, count[0]))

                def carry_wait():
                    nc.vector.tensor_copy(spare[:, 0:1], ident[:, 0:1])

                def moments_of(src):
                    for t in range(T):
                        last = nc.vector.bn_stats(stats[:, t, :], src[:, t, :])
                    step(last)
                    carry_wait()
                    for t in range(T):
                        last = nc.vector.bn_aggr(moments[:, t, :], stats[:, t, :])
                    step(last)
                    v, y, z = root[:, 0, :], root[:, 1, :], root[:, 2, :]
                    step(nc.vector.tensor_scalar(v, moments[:, :, 1], LN_EPS, None, ALU.add))
                    step(nc.vector.tensor_scalar(z.bitcast(i32), v.bitcast(i32), 1, None,
                                                 ALU.logical_shift_right))
                    step(nc.vector.tensor_scalar(y.bitcast(i32), z.bitcast(i32), -1.0, float(0x5f3759df),
                                                 ALU.mult, ALU.add))
                    for r in range(3):
                        step(nc.vector.tensor_tensor(out=z, in0=y, in1=y, op=ALU.mult))
                        step(nc.vector.scalar_tensor_tensor(out=z, in0=z, scalar=-0.5, in1=v,
                                                            op0=ALU.mult, op1=ALU.mult))
                        step(nc.vector.scalar_tensor_tensor(out=(rstd[:] if r == 2 else y), in0=z, scalar=1.5,
                                                            in1=y, op0=ALU.add, op1=ALU.mult))

                def norm_in(k):
                    moments_of(x)
                    for t in range(T):
                        nc.vector.tensor_scalar(xn[:, t, :], x[:, t, :], moments[:, t, 0:1], rstd[:, t:t + 1],
                                                ALU.subtract, ALU.mult).then_inc(xn_ready.sem, 1)

                def norm_out(y, dst):
                    moments_of(y)
                    for t in range(T):
                        last = nc.vector.tensor_scalar(xn[:, t, :], y[:, t, :], moments[:, t, 0:1],
                                                       rstd[:, t:t + 1], ALU.subtract, ALU.mult)
                    step(last)
                    return nc.vector.tensor_tensor(out=dst[:], in0=x[:], in1=xn[:], op=ALU.add)

                y_bank = ps[:, 7, :].rearrange("p (t e) -> p t e", t=T)

                dve.wait_ge(x_loaded.sem, x_loaded.at(b, 16))
                dve.wait_ge(x_final.sem, x_final.at(b, 0))
                nc.vector.tensor_copy(x[:], x_in[:]).then_inc(x_copied.sem, 1)
                dve.wait_ge(x_copied.sem, x_copied.at(b, 1))
                norm_in(0)
                for c in range(H // 2):
                    dve.wait_ge(qrel_ps.sem, qrel_ps.at(b, c + 1))
                    for hh in range(2):
                        rows = slice(hh * RR, (hh + 1) * RR)
                        last = nc.vector.scalar_tensor_tensor(
                            out=q_rel[0:RR, :, 2 * c + hh, :],
                            in0=ps[rows, 3 + c % 3, :].rearrange("p (n i) -> p n i", i=QB),
                            scalar=q_bias_rep[rows, c:c + 1],
                            in1=query_mask[rows, :].unsqueeze(1).broadcast_to([RR, NQB, QB]),
                            op0=ALU.add, op1=ALU.mult)
                    last.then_inc(qrel_ready.sem, 1)

                def copy_pT(n):
                    dve.wait_ge(pT_ps.sem, pT_ps.at(b, n + 1))
                    t, c = n // QPT, n // QPT + 1
                    if t >= 2:
                        dve.wait_ge(av_ps.sem, av_ps.at(b, t - 1))
                    nc.vector.tensor_copy(
                        probsT[t % 2][:, 0:c, :, (n % QPT) * QB:(n % QPT + 1) * QB],
                        ps[:, 4 + n % 2, 0:c * P].rearrange("p (c h i) -> p c h i", h=H, i=QB)
                    ).then_inc(pT_dve.sem, 1)

                def copy_outT(n, av, count):
                    dve.wait_ge(av.sem, av.at(b, count))
                    nc.vector.tensor_copy(outT[:], ps[:, (6 if n < T else 4 + n % 2), :]
                                          ).then_inc(outT_ready.sem, 1)

                def divide_out(n, dst, slots):
                    dve.wait_ge(turned_ps.sem, turned_ps.at(b, n + 1))
                    o = ps[:, 6, :].rearrange("p (k g r) -> p k g r", k=4, g=GH)
                    step(nc.vector.reciprocal(slots, o[:, :, :, D]))
                    nc.vector.tensor_tensor(out=dst, in0=o[:, :, :, 0:D],
                                            in1=slots.unsqueeze(3).broadcast_to([P, 4, GH, D]),
                                            op=ALU.mult).then_inc(attn_ready.sem, 1)

                def divide_tile(t):
                    divide_out(t, attn[:, t, :].rearrange("p (k g d) -> p k g d", g=GH, d=D),
                               den[:, t, :].rearrange("p (k g) -> p k g", g=GH))

                for n in range(NQB):
                    dve.wait_ge(scores_ready.sem, scores_ready.at(b, n + 1))
                    if n >= 8:
                        dve.wait_ge(exp_ready.sem, exp_ready.at(b, n - 7))
                    nc.vector.tensor_reduce(neg_max[:, n % 8:n % 8 + 1], ps[:, n % NB, 0:QB * (n + 1)],
                                            axis=AXX, op=ALU.max, negate=True).then_inc(max_ready.sem, 1)
                    if n >= 3 and (n - 3) % 2 == 0:
                        copy_pT(n - 3)
                    if n == QPT + 5:
                        dve.wait_ge(qwide_ready.sem, qwide_ready.at(b, T))
                    if n >= QPT and n % QPT == 5:
                        copy_outT(n // QPT - 1, av_ps, n // QPT)
                    if n >= QPT and n % QPT == 7:
                        divide_tile(n // QPT - 1)
                copy_pT(NQB - 2)
                copy_outT(T - 1, av_ps, T)
                divide_tile(T - 1)
                dve.wait_ge(y_ready.sem, y_ready.at(b, 1))
                step(norm_out(y_bank, x))

                norm_in(1)
                for f in range(FT):
                    dve.wait_ge(ge_ready.sem, ge_ready.at(b, f + 1))
                    step(nc.vector.tensor_scalar(hid_e[:, f, :], hid_e[:, f, :], 1.0, None, ALU.add))
                    step(nc.vector.reciprocal(hid_e[:, f, :], hid_e[:, f, :]))
                    step(nc.vector.tensor_tensor(out=hid_e[:, f, :], in0=hid_e[:, f, :], in1=ps[:, f, :],
                                                 op=ALU.mult))
                    dve.wait_ge(gu_ps.sem, gu_ps.at(b, 2 * f + 2))
                    nc.vector.tensor_tensor(out=hid[:, f, :], in0=hid_e[:, f, :], in1=ps[:, 3 + f, :],
                                            op=ALU.mult).then_inc(hid_ready.sem, 1)
                dve.wait_ge(y_ready.sem, y_ready.at(b, 2))
                step(norm_out(y_bank, x))

                norm_in(2)
                for w in range(2):
                    dve.wait_ge(qnorm_ready.sem, qnorm_ready.at(b, w + 1))
                    nc.vector.tensor_tensor(out=(qT, kT)[w][:], in0=lin[:, w, :], in1=lin_sq[:, w, :],
                                            op=ALU.mult).then_inc(qk_ready.sem, 1)
                dve.wait_ge(qk_ready.sem, qk_ready.at(b, 2))
                for w, src in enumerate((kT, qT)):
                    step(nc.vector.tensor_copy(halves[:, 2 * w, :], src[:]))
                    step(nc.vector.tensor_tensor(out=halves[:, 2 * w + 1, :], in0=src[:],
                                                 in1=halves[:, 2 * w, :].bitcast(f32), op=ALU.subtract))

                def spread(hg):
                    rows = slice(hg * GR, (hg + 1) * GR)
                    for c in range(4):
                        for dst, part in ((k_parts, c // 2), (q_parts, 2 + c % 2)):
                            last = nc.vector.tensor_copy(dst[c * GR:(c + 1) * GR, hg, :],
                                                         halves[rows, part, :].bitcast(f32))
                    last.then_inc(parts_ready.sem, 1)

                def mask_heads(hg):
                    dve.wait_ge(parts_ready.sem, parts_ready.at(b, hg + 1 if hg == 0 else HG))
                    if hg >= 2:
                        dve.wait_ge(s2_ready.sem, s2_ready.at(b, 2 * GH * (hg - 1)))
                    for g in range(GH):
                        nc.vector.tensor_scalar(q_heads[:, hg % 2, g, :], q_parts[:, hg, :].bitcast(f32),
                                                group_mask[:, g:g + 1], None, ALU.mult
                                                ).then_inc(q_heads_ready.sem, 1)

                spread(0)
                mask_heads(0)
                for hg in range(1, HG):
                    spread(hg)
                mask_heads(1)
                for hg in range(HG):
                    copy_outT(T + hg, av2_ps, 2 * hg + 2)
                    if hg + 2 < HG:
                        mask_heads(hg + 2)
                    divide_out(T + hg, attn[:].rearrange("p t (k g d) -> p t k g d", g=GH, d=D)[:, :, hg, :, :],
                               den[:].rearrange("p t (k g) -> p t k g", g=GH)[:, :, hg, :])
                dve.wait_ge(y_ready.sem, y_ready.at(b, 3))
                step(norm_out(y_bank, x))

                norm_in(3)
                dve.wait_ge(router_ps.sem, router_ps.at(b, 1))
                lg = ps[:, 6, 0:T * NE].rearrange("p (t e) -> p t e", t=T)

                def per_token(a):
                    return a.broadcast_to([P, T, NE])

                step(nc.vector.tensor_reduce(router_s[:, :, 0], lg, axis=AXX, op=ALU.max, negate=True))
                nc.vector.tensor_tensor(out=router[:], in0=lg, in1=per_token(router_s[:, :, 0:1]), op=ALU.add
                                        ).then_inc(router_in.sem, 1)
                dve.wait_ge(router_exp.sem, router_exp.at(b, 1))
                step(nc.vector.tensor_reduce(router_s[:, :, 1], router_e[:], axis=AXX, op=ALU.add))
                step(nc.vector.reciprocal(router_s[:, :, 0], router_s[:, :, 1]))
                step(nc.vector.tensor_tensor(out=router[:], in0=router_e[:], in1=per_token(router_s[:, :, 0:1]),
                                             op=ALU.mult))
                carry_wait()
                for t in range(T):
                    last = nc.vector.max(top8[:, t, :], router[:, t, :])
                step(last)
                carry_wait()
                for t in range(T):
                    last = nc.vector.max_index(top_idx[:, t, :], top8[:, t, :], router[:, t, :])
                step(last)
                step(nc.vector.tensor_copy(top_idx_f[:], top_idx[:]))
                numbers = expert_no[:].unsqueeze(1).broadcast_to([P, T, NE])
                for j, g in enumerate((gates, gates2)):
                    step(nc.vector.tensor_tensor(out=g[:], in0=numbers, in1=per_token(top_idx_f[:, :, j:j + 1]),
                                                 op=ALU.is_equal))
                    step(nc.vector.tensor_tensor(out=g[:], in0=g[:], in1=per_token(top8[:, :, j:j + 1]),
                                                 op=ALU.mult))
                nc.vector.tensor_tensor(out=gates[:], in0=gates[:], in1=gates2[:], op=ALU.add
                                        ).then_inc(gates_ready.sem, 1)
                dve.wait_ge(accb_ps.sem, accb_ps.at(b, 1))
                step(nc.vector.tensor_copy(acc, y_bank))
                for e in range(NE):
                    dve.wait_ge(moe_y_ps.sem, moe_y_ps.at(b, e + 1))
                    for t in range(T):
                        last = nc.vector.scalar_tensor_tensor(
                            out=acc[:, t, :], in0=ps[:, 4 + e % 2, t * P:(t + 1) * P],
                            scalar=gates[:, t, e:e + 1], in1=acc[:, t, :], op0=ALU.mult, op1=ALU.add)
                    last.then_inc(moe_y_used.sem, 1)
                    dve.wait_ge(moe_y_used.sem, moe_y_used.at(b, e + 1))
                dve.wait_ge(x_stored.sem, x_stored.at(b, 0))
                norm_out(acc, x_out).then_inc(x_final.sem, 1)
                assert count[0] == dve_step.per, count[0]

        @block.tensor
        def _(pe):
            mm = nc.tensor.matmul
            pe.wait_ge(consts_ready, 1)
            waited_moe = False
            for n, (kind, a) in enumerate(groups):
                if n == 0:
                    pe.wait_ge(ld_attn, (9 + 2 * QB) * 16)
                    pe.wait_ge(rep_ready, 3)
                if n == 1:
                    pe.wait_ge(wf_ready, 1)
                if n == first_moe:
                    pe.wait_ge(ld_moe, 5 * 16)
                if n >= PREP_BANKS:
                    ca, cd = copies(n - PREP_BANKS)
                    if ca:
                        pe.wait_ge(prep_act, ca)
                    if cd:
                        pe.wait_ge(prep_dve, cd)
                bank = ps[:, n % PREP_BANKS, :]
                if kind == "rel":
                    for c in range(NREL // P):
                        last = mm(bank[0:RR, c * P:(c + 1) * P],
                                  rel_rep[:, c, :, :], ident[:], start=True, stop=True)
                elif kind in ("gate_up", "down"):
                    for f in range(FT):
                        last = nc.tensor.transpose(bank[:, f * P:(f + 1) * P],
                                                   wf_in[:, a, f * P:(f + 1) * P], ident[:])
                elif kind == "small":
                    nc.tensor.transpose(bank[:, 0:NE], gate_in, ident[0:NE, 0:NE])
                    for m in range(MF):
                        last = nc.tensor.transpose(bank[:, NE * (m + 1):NE * (m + 2)],
                                                   b1_in[:, m * P:(m + 1) * P], ident[0:NE, 0:NE])
                elif kind == "w1":
                    for m in range(MF):
                        last = nc.tensor.transpose(bank[:, m * P:(m + 1) * P], w1_in[:, m, a, :], ident[:])
                else:
                    for m in range(MF):
                        last = nc.tensor.transpose(bank[:, m * P:(m + 1) * P],
                                                   w2_in[:, a, m * P:(m + 1) * P], ident[:])
                last.then_inc(prep_done, 1)
            pe.wait_ge(prep_act, (len(groups) + 1) // 2)
            pe.wait_ge(prep_dve, len(groups) // 2)
            pe.wait_ge(j_ready, 2)
            pe.wait_ge(qb_ready, 8)
            row = qbias_row[:].rearrange("a m c o -> a m (c o)")
            for m in range(2):
                mm(ps[:, 7, 2 + m:3 + m], row[:, m, :], ones[:, 0:1], start=True, stop=True)
            mm(ps[:, 7, 0:1], ones[:], j_sum[:], start=True, stop=True).then_inc(j_ready, 1)
            pe.wait_ge(j_ready, 5)
            pe.wait_ge(toep_dma, 16 * QB)

            with pe.Fori(0, B) as b:
                def input_T(k):
                    for t in range(T):
                        pe.wait_ge(xn_ready.sem, xn_ready.at(b, k * T + t + 1))
                        last = nc.tensor.transpose(ps[:, 6, t * P:(t + 1) * P], xn[:, t, :], ident[:])
                    last.then_inc(xnT_ps.sem, 1)
                    pe.wait_ge(xnT_ready.sem, xnT_ready.at(b, k + 1))

                def token_major(bank, t, w, bias, src):
                    o = ps[:, bank, t * P:(t + 1) * P]
                    mm(o, src[:, t * P:(t + 1) * P], w, start=True, stop=False)
                    return mm(o, ones[:], bias, start=False, stop=True)

                input_T(0)
                mm(ps[:, 0, :], w_qkvo[:, 0, :], xnT[:], start=True, stop=True).then_inc(proj_ps.sem, 1)
                mm(ps[:, 1, :], w_qkvo[:, 1, :], xnT[:], start=True, stop=True).then_inc(proj_ps.sem, 1)
                for t in range(T):
                    last = token_major(2, t, w_qkvo[:, 2, :], bias_rows[:, 0, :], xnT)
                last.then_inc(proj_ps.sem, 1)
                for c in range(H // 2):
                    if c >= 3:
                        pe.wait_ge(qrel_ready.sem, qrel_ready.at(b, c - 2))
                    mm(ps[:, 3 + c % 3, :], wq_rep[:, c, :, :, :], xnT[:], start=True, stop=True
                       ).then_inc(qrel_ps.sem, 1)
                pe.wait_ge(qrel_ready.sem, qrel_ready.at(b, H // 2))
                pe.wait_ge(proj_copied.sem, proj_copied.at(b, 3))

                def scores(n):
                    if n % QPT == 0:
                        pe.wait_ge(qwide_ready.sem, qwide_ready.at(b, n // QPT + 1))
                    if n >= NB:
                        pe.wait_ge(exp_ready.sem, exp_ready.at(b, n - NB + 1))
                    L = QB * (n + 1)
                    o = ps[:, n % NB, 0:L]
                    mm(o, q_wide0[:, n, :, :], kT[:, 0:L], start=True, stop=False)
                    mm(o, q_rel[:, n, :, :], toep[:, S - L:S], start=False, stop=True
                       ).then_inc(scores_ready.sem, 1)

                def transpose_probs(n):
                    pe.wait_ge(exp_ready.sem, exp_ready.at(b, n + 1))
                    if n >= 2:
                        done = (pT_dve, pT_act)[n % 2]
                        pe.wait_ge(done.sem, done.at(b, n // 2))
                    for c in range(n // QPT + 1):
                        last = nc.tensor.transpose(ps[:, 4 + n % 2, c * P:(c + 1) * P],
                                                   probs[:, n % NB, c * P:(c + 1) * P], ident[:])
                    last.then_inc(pT_ps.sem, 1)

                def weigh_values(t):
                    pe.wait_ge(pT_dve.sem, pT_dve.at(b, (t + 1) * QPT // 2))
                    pe.wait_ge(pT_act.sem, pT_act.at(b, (t + 1) * QPT // 2))
                    for k in range(HG):
                        for c in range(t + 1):
                            for g in range(GH):
                                h = k * GH + g
                                last = mm(ps[32 * g:32 * g + D + 1, 6, k * P:(k + 1) * P],
                                          v_ones[:, c, h, :], probsT[t % 2][:, c, h, :],
                                          start=(c == 0), stop=(c == t))
                    last.then_inc(av_ps.sem, 1)

                def turn_out(n):
                    pe.wait_ge(outT_ready.sem, outT_ready.at(b, n + 1))
                    if n > T:
                        pe.wait_ge(attn_ready.sem, attn_ready.at(b, n))
                    for k in range(4):
                        last = nc.tensor.transpose(ps[:, 6, k * P:(k + 1) * P], outT[:, k * P:(k + 1) * P],
                                                   ident[:])
                    last.then_inc(turned_ps.sem, 1)

                def attn_T(t):
                    pe.wait_ge(attn_ready.sem, attn_ready.at(b, t + 1))
                    nc.tensor.transpose(ps[:, 6, 256:256 + P], attn[:, t, :], ident[:]
                                        ).then_inc(attnT_ps.sem, 1)

                def project(t):
                    pe.wait_ge(attnT_ready.sem, attnT_ready.at(b, t + 1))
                    return token_major(7, t, w_qkvo[:, 3, :], bias_rows[:, 1, :], attnT)

                for n in range(3):
                    scores(n)
                for n in range(NQB):
                    if n + 3 < NQB:
                        scores(n + 3)
                    transpose_probs(n)
                    t = n // QPT - 1
                    if t >= 0 and n % QPT == 3:
                        weigh_values(t)
                    if t >= 0 and n % QPT == 5:
                        turn_out(t)
                    if t >= 0 and n % QPT == 8:
                        attn_T(t)
                    if t >= 0 and n % QPT == 10:
                        project(t)
                weigh_values(T - 1)
                turn_out(T - 1)
                attn_T(T - 1)
                project(T - 1).then_inc(y_ready.sem, 1)

                input_T(1)
                for f in range(FT):
                    mm(ps[:, f, :], wgT[:, f * P:(f + 1) * P], xnT[:], start=True, stop=True
                       ).then_inc(gu_ps.sem, 1)
                    mm(ps[:, 3 + f, :], wuT[:, f * P:(f + 1) * P], xnT[:], start=True, stop=True
                       ).then_inc(gu_ps.sem, 1)
                pe.wait_ge(hid_ready.sem, hid_ready.at(b, FT))
                for t in range(T):
                    for f in range(FT):
                        last = mm(ps[:, 7, t * P:(t + 1) * P], hid[:, f, t * P:(t + 1) * P], wdT[:, f, :],
                                  start=(f == 0), stop=(f == FT - 1))
                last.then_inc(y_ready.sem, 1)

                input_T(2)
                wq2 = w_quat[:].rearrange("p m c o -> p m (c o)")
                for w in range(2):
                    mm(ps[:, w, :], wq2[:, w, :], xnT[:], start=True, stop=True).then_inc(proj_ps.sem, 1)
                for t in range(T):
                    last = token_major(2, t, wq2[:, 2, :], row[:, 2, :], xnT)
                last.then_inc(proj_ps.sem, 1)
                for w in range(2):
                    pe.wait_ge(proj_copied.sem, proj_copied.at(b, 3 + 2 * (w + 1)))
                    mm(ps[:, 3 + w, :], same_part[:], lin_sq[:, w, :], start=True, stop=True
                       ).then_inc(norm_ps.sem, 1)
                pe.wait_ge(proj_copied.sem, proj_copied.at(b, 8))
                pe.wait_ge(qk_ready.sem, qk_ready.at(b, 2))

                def scores2(n, g):
                    hg, a, i = n // 2, n % 2, n * GH + g
                    if a == 0:
                        pe.wait_ge(q_heads_ready.sem, q_heads_ready.at(b, hg * GH + g + 1))
                    if i >= 2:
                        pe.wait_ge(e2_ready.sem, e2_ready.at(b, i - 1))
                    for c in range(2):
                        key = (2 * a + c) * P
                        last = mm(ps[:, 2 * (i % 2) + c, :], k_parts[:, hg, key:key + P],
                                  q_heads[:, hg % 2, g, :], start=True, stop=True)
                    last.then_inc(s2_ready.sem, 1)

                def weigh_values2(n):
                    hg, a = n // 2, n % 2
                    pe.wait_ge(e2_ready.sem, e2_ready.at(b, (n + 1) * GH))
                    if hg >= 2 and a == 0:
                        pe.wait_ge(outT_ready.sem, outT_ready.at(b, T + hg - 1))
                    for c in range(2):
                        for g in range(GH):
                            last = mm(ps[32 * g:32 * g + D + 1, 4 + hg % 2, :], v_ones[:, 2 * a + c, hg * GH + g, :],
                                      head_probs[:, n % 2, g, c, :], start=(a == 0 and c == 0),
                                      stop=(a == 1 and c == 1))
                    last.then_inc(av2_ps.sem, 1)

                for n in range(2 * HG):
                    for g in range(GH):
                        scores2(n, g)
                        if g == 1 and n >= 1:
                            weigh_values2(n - 1)
                        if g == 3 and n >= 3 and n % 2:
                            turn_out(T + n // 2 - 1)
                weigh_values2(2 * HG - 1)
                turn_out(T + HG - 1)
                for t in range(T):
                    pe.wait_ge(attn_ready.sem, attn_ready.at(b, T + HG))
                    last = nc.tensor.transpose(ps[:, 6, t * P:(t + 1) * P], attn[:, t, :], ident[:])
                last.then_inc(attnT_ps.sem, 1)
                pe.wait_ge(attnT_ready.sem, attnT_ready.at(b, T + 1))
                for t in range(T):
                    last = token_major(7, t, wq2[:, 3, :], row[:, 3, :], attnT)
                last.then_inc(y_ready.sem, 1)

                input_T(3)
                for t in range(T):
                    last = mm(ps[:, 6, t * NE:(t + 1) * NE], xnT[:, t * P:(t + 1) * P], gateT[:],
                              start=True, stop=True)
                last.then_inc(router_ps.sem, 1)

                def expert_up(e):
                    for m in range(MF):
                        n = e * MF + m
                        if n >= NB:
                            pe.wait_ge(moe_h_ready.sem, moe_h_ready.at(b, n - NB + 1))
                        mm(ps[:, n % NB, :], w1T[:, e, m * P:(m + 1) * P], xnT[:], start=True, stop=True
                           ).then_inc(moe_h_ps.sem, 1)

                def expert_down(e):
                    pe.wait_ge(moe_h_ready.sem, moe_h_ready.at(b, (e + 1) * MF))
                    if e >= 2:
                        pe.wait_ge(moe_y_used.sem, moe_y_used.at(b, e - 1))
                    for t in range(T):
                        for m in range(MF):
                            last = mm(ps[:, 4 + e % 2, t * P:(t + 1) * P],
                                      moe_h[:, e % 2, m, t * P:(t + 1) * P], w2T[:, m, e, :],
                                      start=(m == 0), stop=(m == MF - 1))
                    last.then_inc(moe_y_ps.sem, 1)

                expert_up(0)
                pe.wait_ge(gates_ready.sem, gates_ready.at(b, 1))
                for t in range(T):
                    last = nc.tensor.transpose(ps[0:NE, 7, t * P:(t + 1) * P], gates[:, t, :], ident[:])
                last.then_inc(gatesT_ps.sem, 1)
                pe.wait_ge(gatesT_ready.sem, gatesT_ready.at(b, 1))
                for t in range(T):
                    last = mm(ps[:, 7, t * P:(t + 1) * P], gates_T[:, t, :], b2_sb[:], start=True, stop=True)
                last.then_inc(accb_ps.sem, 1)
                for e in range(NE):
                    if e + 1 < NE:
                        expert_up(e + 1)
                    expert_down(e)


_INS = ['L0_attn_x', 'L0_attn_Wq', 'L0_attn_bq', 'L0_attn_Wk', 'L0_attn_bk', 'L0_attn_Wv', 'L0_attn_bv',
        'L0_attn_Wo', 'L0_attn_bo', 'L0_attn_rel_key', 'L0_ffn_w_gate', 'L0_ffn_w_up', 'L0_ffn_w_down',
        'L1_attn_qW', 'L1_attn_qb', 'L1_attn_kW', 'L1_attn_kb', 'L1_attn_vW', 'L1_attn_vb', 'L1_attn_oW',
        'L1_attn_ob', 'L1_attn_J', 'L1_ffn_gate_w', 'L1_ffn_w1', 'L1_ffn_b1', 'L1_ffn_w2', 'L1_ffn_b2']


def kernel(**inputs):
    import numpy as _np
    import concourse.bacc as _bacc
    from concourse import mybir as _mybir
    from concourse.bass_utils import run_bass_kernel_spmd as _run

    nc = _bacc.Bacc("TRN2", target_bir_lowering=False, num_devices=1)
    arrays, args = {}, []
    for name in _INS:
        a = _np.ascontiguousarray(inputs[name])
        arrays[f"in_{name}_dram"] = a
        args.append(nc.dram_tensor(f"in_{name}_dram", a.shape, _mybir.dt.from_np(a.dtype), kind="ExternalInput").ap())
    shape = _np.shape(inputs['L0_attn_x'])
    o = nc.dram_tensor("out_dram", shape, _mybir.dt.float32, kind="ExternalOutput").ap()
    build_sandwich(nc, *args, o)
    r = _run(nc, [arrays], core_ids=[0])
    return r.results[0]["out_dram"]
```

```python
import numpy as np
import concourse.bass as bass
from concourse import mybir
from contextlib import ExitStack


class Signal:

    def __init__(self, sem, per, base=0):
        self.sem, self.per, self.base = sem, per, base

    def at(self, batch, n):
        return batch * self.per + (self.base + n)


def build_sandwich(nc, X, Wq, bq, Wk, bk, Wv, bv, Wo, bo, rel_key, w_gate, w_up, w_down,
                   qW, qb, kW, kb, vW, vb, oW, ob, J, gate_w, w1, b1, w2, b2, out):
    f32, f32r, i32, u32 = mybir.dt.float32, mybir.dt.float32r, mybir.dt.int32, mybir.dt.uint32
    ALU = mybir.AluOpType
    ACT = mybir.ActivationFunctionType
    AXX = mybir.AxisListType.X

    B, S, E = X.shape
    P = 128
    T = S // P
    NREL, D = rel_key.shape
    H = E // D
    QB = P // H
    NQB = S // QB
    QPT = P // QB
    RR = QB * D
    HID = w_gate.shape[0]
    FT = HID // P
    NF, NE, _ = w1.shape
    MF = NF // P
    GH = 4
    HG = H // GH
    GR = GH * D
    QD = E // 4
    SCALE = float(D) ** -0.5
    DEQ = 1.0 / 127.0
    LN_EPS, QN_EPS = 1e-5, 1e-6
    MASKED = -1e30
    TWO_PI = 2.0 * np.pi
    NB = 4

    ctx = ExitStack()
    with ctx:
        nc.disable_value_cache = True

        def sb(name, shape, dt=f32):
            return ctx.enter_context(nc.sbuf_tensor(name, shape, dt))

        def sem(name):
            return ctx.enter_context(nc.semaphore(name))

        ident = sb("ident", [P, P])
        ones = sb("ones", [1, P])
        group_mask = sb("group_mask", [P, GH])
        head_mask = sb("head_mask", [P, H])
        query_mask = sb("query_mask", [P, QB])
        same_part = sb("same_part", [P, P])
        signs = sb("signs", [P, 4])
        eps_col = sb("eps_col", [P, 1])
        spare = sb("spare", [P, 4])
        unit = sb("unit", [P, 1])
        expert_no = sb("expert_no", [P, NE])
        toep = sb("toep", [RR + QB, S])
        rel_rows = sb("rel_rows", [RR, NREL])
        w_qkvo = sb("w_qkvo", [P, 4, P])
        q_bias = sb("q_bias", [P, 1])
        k_bias = sb("k_bias", [P, 1])
        wq_rep = sb("wq_rep", [P, H // 2, 2, QB, D])
        far_bias = sb("far_bias", [P, 1])
        q_bias_rep = sb("q_bias_rep", [P, H // 2])
        bias_rows = sb("bias_rows", [1, 2, P])
        rel_in = sb("rel_in", [P, NREL // P, D])
        wgT = sb("wgT", [P, HID])
        wuT = sb("wuT", [P, HID])
        wdT = sb("wdT", [P, FT, P])
        w_quat = sb("w_quat", [P, 4, 4, QD])
        qbias_in = sb("qbias_in", [1, 4, 4, QD])
        qbias_row = sb("qbias_row", [1, 4, 4, QD])
        qbias_col = sb("qbias_col", [P, 2])
        j_row = sb("j_row", [1, P])
        j_turn = sb("j_turn", [1, P])
        j_sum = sb("j_sum", [1, 1])
        j_bias = sb("j_bias", [P, 1])
        w1T = sb("w1T", [P, NE, NF])
        w2T = sb("w2T", [P, MF, NE, P])
        gateT = sb("gateT", [P, NE])
        b1T = sb("b1T", [P, MF, NE])
        b2_sb = sb("b2_sb", [NE, P])
        x_in = sb("x_in", [P, T, E])
        x = sb("x", [P, T, E])
        stats = sb("stats", [P, T, 6])
        moments = sb("moments", [P, T, 2])
        rstd = sb("rstd", [P, T])
        y_moments = sb("y_moments", [P, T, 2])
        y_rstd = sb("y_rstd", [P, T])
        root = sb("root", [P, 3, T])
        xn = sb("xn", [P, T, E])
        xnT = sb("xnT", [P, S])
        qT = sb("qT", [P, S])
        kT = sb("kT", [P, S])
        kT_far = sb("kT_far", [P, S])
        head_T = sb("head_T", [P, S])
        v_ones = sb("v_ones", [P, T, H, D + 1])
        with ExitStack() as shared:
            k_parts = shared.enter_context(nc.sbuf_tensor("k_parts", [P, HG, S], f32r))
            q_parts = shared.enter_context(nc.sbuf_tensor("q_parts", [P, HG, S], f32r))
            q_heads = shared.enter_context(nc.sbuf_tensor("q_heads", [P, 2, GH, S], f32r))
        q_wide = sb("q_wide", [P, NQB * H * QB])
        halves = q_heads[:, 1, :, :]
        q_rel = sb("q_rel", [RR + QB, NQB, H, QB])
        probs = sb("probs", [P, NB, S])
        pT_all = sb("pT_all", [P, (2 * T - 1) * H * P])
        neg_max = sb("neg_max", [P, 8])
        den = sb("den", [P, T, H])
        attn = xn
        attnT = xnT
        q_wide0 = q_wide[:].rearrange("p (n h i) -> p n h i", h=H, i=QB)
        pT_flat = pT_all[:]
        pT_odd = (T - 1) * H * P
        probsT = [pT_flat[:, 0:pT_odd].rearrange("p (c h i) -> p c h i", c=T - 1, h=H),
                  pT_flat[:, pT_odd:].rearrange("p (c h i) -> p c h i", c=T, h=H)]
        w1_in = pT_flat[:, 0:MF * NE * P].rearrange("p (m e d) -> p m e d", m=MF, e=NE)
        w2_in = pT_flat[:, MF * NE * P:2 * MF * NE * P].rearrange("p (e f) -> p e f", e=NE)
        o0 = 2 * MF * NE * P
        wi_in = pT_flat[:, o0:o0 + 3 * HID].bitcast(i32).rearrange("p (w n) -> p w n", w=3)
        wf_in = pT_flat[:, o0 + 3 * HID:o0 + 6 * HID].rearrange("p (w n) -> p w n", w=3)
        b1_in = pT_flat[0:NE, o0 + 6 * HID:o0 + 6 * HID + NF]
        gate_in = pT_flat[0:NE, o0 + 6 * HID + NF:o0 + 6 * HID + NF + P]
        rel_rep = pT_flat[:, o0 + 6 * HID + NF + P:o0 + 6 * HID + NF + P + RR * NREL // P].rearrange(
            "p (a i d) -> p a i d", a=NREL // P, i=QB)
        hp = 2 * GH * 2 * S
        r0 = o0 + 6 * HID + NF + P + RR * NREL // P
        rel_first = pT_flat[:, r0:r0 + P].rearrange("p (h d) -> p h d", h=H)
        head_probs = pT_flat[:, 0:hp].rearrange("p (a g c s) -> p a g c s", a=2, g=GH, c=2)
        lin = pT_flat[:, hp:hp + 2 * S].rearrange("p (w s) -> p w s", w=2)
        lin_sq = pT_flat[:, hp + 2 * S:hp + 4 * S].rearrange("p (w s) -> p w s", w=2)
        outT = qT
        hid_e = pT_flat[:, 0:FT * S].rearrange("p (f s) -> p f s", f=FT)
        hid = pT_flat[:, FT * S:2 * FT * S].rearrange("p (f s) -> p f s", f=FT)
        moe_h = pT_flat[:, 0:2 * MF * S].rearrange("p (a f s) -> p a f s", a=2, f=MF)
        acc = pT_flat[:, 2 * MF * S:2 * MF * S + T * E].rearrange("p (t d) -> p t d", t=T)
        x_out = pT_flat[:, 2 * MF * S + T * E:2 * MF * S + 2 * T * E].rearrange("p (t d) -> p t d", t=T)
        y_out = pT_flat[:, 2 * MF * S + 2 * T * E:2 * MF * S + 3 * T * E].rearrange("p (t d) -> p t d", t=T)
        router = sb("router", [P, T, NE])
        router_e = sb("router_e", [P, T, NE])
        router_s = sb("router_s", [P, T, 2])
        top8 = sb("top8", [P, T, 8])
        top_idx = sb("top_idx", [P, T, 8], u32)
        top_idx_f = sb("top_idx_f", [P, T, 8])
        gates = sb("gates", [P, T, NE])
        gates2 = sb("gates2", [P, T, NE])
        gates_T = sb("gates_T", [NE, T, P])

        ps = ctx.enter_context(nc.psum_tensor("ps", [P, 8, 512], f32))

        ld_attn, ld_ffn, ld_quat, ld_moe = sem("ld_attn"), sem("ld_ffn"), sem("ld_quat"), sem("ld_moe")
        ld_rows = sem("ld_rows")
        ld_bias = sem("ld_bias")
        toep_dma = sem("toep_dma")
        pool_step = sem("pool_step")
        consts_early = sem("consts_early")
        consts_ready = sem("consts_ready")
        prep_done = sem("prep_done")
        prep_act = sem("prep_act")
        prep_dve = sem("prep_dve")
        rep_ready = sem("rep_ready")
        wf_ready = sem("wf_ready")
        prep_chain = sem("prep_chain")
        j_ready = sem("j_ready")
        toep_base = sem("toep_base")
        qb_ready = sem("qb_ready")
        x_loaded = Signal(sem("x_loaded"), 16)
        x_copied = Signal(sem("x_copied"), 1, base=1)
        x_final = Signal(sem("x_final"), 1, base=1)
        x_stored = Signal(sem("x_stored"), 16, base=16)
        dve_step = Signal(sem("dve_step"), 112)
        xn_ready = Signal(sem("xn_ready"), 3 * T)
        xnT_ps = Signal(sem("xnT_ps"), 3)
        xnT_ready = Signal(sem("xnT_ready"), 3)
        head_step = Signal(sem("head_step"), 11)
        head_xn = Signal(sem("head_xn"), T)
        head_xT_ps = Signal(sem("head_xT_ps"), 1)
        head_xT = Signal(sem("head_xT"), 1)
        head_proj_ps = Signal(sem("head_proj_ps"), 3)
        head_proj = Signal(sem("head_proj"), 4)
        y_ready = Signal(sem("y_ready"), 3)
        proj_ps = Signal(sem("proj_ps"), 3)
        proj_copied = Signal(sem("proj_copied"), 5)
        qrel_ps = Signal(sem("qrel_ps"), H // 2)
        qrel_ready = Signal(sem("qrel_ready"), H // 2)
        qwide_ready = Signal(sem("qwide_ready"), T)
        probs_zero = Signal(sem("probs_zero"), 1)
        scores_ready = Signal(sem("scores_ready"), NQB)
        max_ready = Signal(sem("max_ready"), NQB)
        exp_ready = Signal(sem("exp_ready"), NQB)
        pT_ps = Signal(sem("pT_ps"), NQB)
        pT_dve = Signal(sem("pT_dve"), NQB // 2)
        pT_act = Signal(sem("pT_act"), NQB // 2)
        av_ps = Signal(sem("av_ps"), T)
        outT_ready = Signal(sem("outT_ready"), T + HG)
        turned_ps = Signal(sem("turned_ps"), T + HG)
        attn_ready = Signal(sem("attn_ready"), T + HG)
        attnT_ps = Signal(sem("attnT_ps"), T + 1)
        attnT_ready = Signal(sem("attnT_ready"), T + 1)
        gu_ps = Signal(sem("gu_ps"), 2 * FT)
        ge_ready = Signal(sem("ge_ready"), FT)
        hid_ready = Signal(sem("hid_ready"), FT)
        norm_ps = Signal(sem("norm_ps"), 2)
        qnorm_ready = Signal(sem("qnorm_ready"), 2)
        act_step = Signal(sem("act_step"), 2)
        qk_ready = Signal(sem("qk_ready"), 2)
        halves_ready = Signal(sem("halves_ready"), 1)
        k_first_ready = Signal(sem("k_first_ready"), 1)
        k_rest_ready = Signal(sem("k_rest_ready"), 4 * (HG - 1))
        q_parts_ready = Signal(sem("q_parts_ready"), HG)
        q_heads_ready = Signal(sem("q_heads_ready"), H)
        s2_ready = Signal(sem("s2_ready"), 2 * H)
        e2_ready = Signal(sem("e2_ready"), 2 * H)
        av2_ps = Signal(sem("av2_ps"), 2 * HG)
        router_ps = Signal(sem("router_ps"), 1)
        router_in = Signal(sem("router_in"), 1)
        router_exp = Signal(sem("router_exp"), 1)
        gates_ready = Signal(sem("gates_ready"), 1)
        gatesT_ps = Signal(sem("gatesT_ps"), 1)
        gatesT_ready = Signal(sem("gatesT_ready"), 1)
        accb_ps = Signal(sem("accb_ps"), 1)
        acc_ready = Signal(sem("acc_ready"), 1)
        moe_h_ps = Signal(sem("moe_h_ps"), NE * MF)
        moe_h_ready = Signal(sem("moe_h_ready"), NE * MF)
        moe_y_ps = Signal(sem("moe_y_ps"), NE)
        moe_y_used = Signal(sem("moe_y_used"), NE)

        MATS = [qW, kW, vW, oW]
        QBIAS = [qb, kb, vb, ob]
        PREP_BANKS = 6

        block = ctx.enter_context(nc.Block())

        @block.sync
        def _(sp):
            def load_x(src):
                sp.dma_start(x_in[:], src.rearrange("a (t p) e -> p (a t) e", p=P)).then_inc(x_loaded.sem, 16)

            def store_x(dst):
                sp.dma_start(dst.rearrange("a (t p) e -> p (a t) e", p=P), x_out).then_inc(x_stored.sem, 16)

            for j, w in enumerate((Wq, Wk, Wv, Wo)):
                sp.dma_start(w_qkvo[:, j, :], w).then_inc(ld_attn, 16)
            sp.dma_start(rel_in[:], rel_key.rearrange("(a p) d -> p a d", p=P)).then_inc(ld_attn, 16)
            load_x(X[0:1])
            sp.dma_start(q_bias[:], bq.rearrange("(p a) -> p a", a=1)).then_inc(ld_attn, 16)
            sp.dma_start(k_bias[:], bk.rearrange("(p a) -> p a", a=1)).then_inc(ld_attn, 16)
            sp.dma_start(bias_rows[:, 0, :], bv.rearrange("(a p) -> a p", a=1)).then_inc(ld_attn, 16)
            sp.dma_start(bias_rows[:, 1, :], bo.rearrange("(a p) -> a p", a=1)).then_inc(ld_attn, 16)
            for m, w in enumerate(QBIAS):
                sp.dma_start(qbias_in[:, m, :, :], w.rearrange("(a w) o -> a w o", a=1)).then_inc(ld_rows, 16)
            sp.dma_start(j_row[:], J.rearrange("(a p) -> a p", a=1)).then_inc(ld_rows, 16)
            for hh in range(2):
                for i in range(QB):
                    sp.dma_start(q_bias_rep[hh * RR + i * D:hh * RR + (i + 1) * D, :],
                                 bq.rearrange("(c z d) -> z d c", z=2, d=D)[hh],
                                 allow_slow_non_contiguous=True).then_inc(ld_bias, 16)
            sp.dma_start(wi_in[:, 0, :].rearrange("p (f d) -> p f d", f=FT),
                         w_gate.rearrange("(f p) d -> p f d", p=P)).then_inc(ld_ffn, 16)
            sp.dma_start(wi_in[:, 1, :].rearrange("p (f d) -> p f d", f=FT),
                         w_up.rearrange("(f p) d -> p f d", p=P)).then_inc(ld_ffn, 16)
            sp.dma_start(wi_in[:, 2, :], w_down).then_inc(ld_ffn, 16)
            sp.dma_start(gate_in, gate_w).then_inc(ld_moe, 16)
            sp.dma_start(b1_in, b1).then_inc(ld_moe, 16)
            sp.dma_start(b2_sb[:], b2).then_inc(ld_moe, 16)
            sp.dma_start(w1_in, w1.rearrange("(m p) e d -> p m e d", p=P)).then_inc(ld_moe, 16)
            sp.dma_start(w2_in, w2).then_inc(ld_moe, 16)
            for m, w in enumerate(MATS):
                for c in range(4):
                    rows = slice(c * QD, (c + 1) * QD)
                    for p0, n, by in ([(0, 4, 1)], [(0, 2, 2), (1, 2, 2)], [(0, 2, 1), (2, 2, 1)],
                                      [(i, 1, 1) for i in range(4)])[c]:
                        w0 = c ^ p0
                        sp.dma_start(w_quat[rows, m, p0:p0 + (n - 1) * by + 1:by, :],
                                     w[w0:w0 + (n - 1) * by + 1:by].rearrange("w d o -> d w o")
                                     ).then_inc(ld_quat, 16)
            with sp.Fori(0, B - 1) as b:
                sp.wait_ge(x_copied.sem, x_copied.at(b, 1))
                load_x(X[bass.ds(b + 1, 1)])
                sp.wait_ge(x_final.sem, x_final.at(b, 1))
                store_x(out[bass.ds(b, 1)])
            sp.wait_ge(x_copied.sem, B + 1)
            load_x(X[0:1])
            sp.wait_ge(x_final.sem, B + 1)
            store_x(out[B - 1:B])
            sp.wait_ge(x_stored.sem, 16 * (B + 1))

        @block.gpsimd
        def _(pool):
            done = [0]

            def step(ins):
                done[0] += 1
                ins.then_inc(pool_step, 1)
                pool.wait_ge(pool_step, done[0])

            step(pool.memset(ident[:], 0.0))
            step(pool.affine_select(out=ident[:], in_=ident[:], compare_op=ALU.not_equal, fill=1.0,
                                    base=0, pattern=[[-1, P]], channel_multiplier=1))
            step(pool.memset(ones[:], 1.0))
            step(pool.memset(eps_col[:], QN_EPS))
            step(pool.memset(unit[:], 1.0))
            step(pool.memset(head_mask[:], SCALE))
            step(pool.affine_select(out=head_mask[:], in_=head_mask[:], compare_op=ALU.is_ge, fill=0.0,
                                    base=0, pattern=[[-D, H]], channel_multiplier=1))
            step(pool.affine_select(out=head_mask[:], in_=head_mask[:], compare_op=ALU.is_ge, fill=0.0,
                                    base=D - 1, pattern=[[D, H]], channel_multiplier=-1))
            step(pool.memset(query_mask[:], SCALE))
            for r in (0, RR):
                m = query_mask[r:r + RR, :]
                step(pool.affine_select(out=m, in_=m, compare_op=ALU.is_ge, fill=0.0,
                                        base=0, pattern=[[-D, QB]], channel_multiplier=1))
                step(pool.affine_select(out=m, in_=m, compare_op=ALU.is_ge, fill=0.0,
                                        base=D - 1, pattern=[[D, QB]], channel_multiplier=-1))
            pool.memset(v_ones[:], 1.0).then_inc(consts_early, 1)
            pool.wait_ge(consts_early, 1)
            step(pool.memset(group_mask[:], SCALE))
            for r in range(0, P, GR):
                m = group_mask[r:r + GR, :]
                step(pool.affine_select(out=m, in_=m, compare_op=ALU.is_ge, fill=0.0,
                                        base=0, pattern=[[-D, GH]], channel_multiplier=1))
                step(pool.affine_select(out=m, in_=m, compare_op=ALU.is_ge, fill=0.0,
                                        base=D - 1, pattern=[[D, GH]], channel_multiplier=-1))
            step(pool.memset(same_part[:], 0.0))
            for k in range(-3, 4):
                step(pool.affine_select(out=same_part[:], in_=same_part[:], compare_op=ALU.not_equal, fill=1.0,
                                        base=k * QD, pattern=[[-1, P]], channel_multiplier=1))
            step(pool.memset(signs[:], 1.0))
            for c, part in ((1, 0), (2, 0), (3, 0), (2, 1), (3, 2), (1, 3)):
                step(pool.memset(signs[c * QD:(c + 1) * QD, part:part + 1], -1.0))
            step(pool.iota(expert_no[:], [[1, NE]], base=0, channel_multiplier=0,
                           allow_small_or_imprecise_dtypes=True))
            step(pool.memset(toep[RR:RR + QB, :], 0.0))
            pool.affine_select(out=toep[RR:RR + QB, :], in_=toep[RR:RR + QB, :], compare_op=ALU.is_ge,
                               fill=MASKED, base=S - QB, pattern=[[-1, S]], channel_multiplier=1
                               ).then_inc(consts_ready, 1)
            pool.wait_ge(consts_ready, 1)

            def head(b, ahead):
                pool.wait_ge(head_proj.sem, head_proj.at(b, ahead * head_proj.per + 1))
                for t in range(T):
                    blocks = slice(t * QPT, (t + 1) * QPT)
                    q_in = qT[:, t * P:(t + 1) * P].rearrange("p (n i) -> p n i", i=QB)
                    if t == 1:
                        pool.memset(probs[:], 0.0).then_inc(probs_zero.sem, 1)
                    pool.tensor_tensor(
                        out=q_wide0[:, blocks, :, :],
                        in0=q_in.unsqueeze(2).broadcast_to([P, QPT, H, QB]),
                        in1=head_mask[:].unsqueeze(1).unsqueeze(3).broadcast_to([P, QPT, H, QB]),
                        op=ALU.mult).then_inc(qwide_ready.sem, 1)

            head(0, 0)
            with pool.Fori(0, B) as b:
                pool.wait_ge(halves_ready.sem, halves_ready.at(b, 1))
                pool.wait_ge(qwide_ready.sem, qwide_ready.at(b, T))
                for n in range(4 * (HG - 1)):
                    hg, c = n // 4 + 1, n % 4
                    rows = slice(hg * GR, (hg + 1) * GR)
                    pool.tensor_tensor(out=k_parts[c * GR:(c + 1) * GR, hg, :],
                                       in0=halves[rows, c // 2, :].bitcast(f32),
                                       in1=unit[rows, :].broadcast_to([GR, S]), op=ALU.mult
                                       ).then_inc(k_rest_ready.sem, 1)
                    pool.wait_ge(k_rest_ready.sem, k_rest_ready.at(b, n + 1))
                head(b, 1)

        def prep_groups():
            yield ("rel", None)
            yield ("gate_up", 0)
            yield ("gate_up", 1)
            yield ("down", 2)
            yield ("small", None)
            for e in range(NE):
                yield ("w1", e)
                yield ("w2", e)
        groups = list(prep_groups())
        first_moe = 4

        def prep_copy(eng, copy, which, first=0, end=99):
            for n, (kind, a) in enumerate(groups):
                if n % 2 != which or not first <= n < end:
                    continue
                eng.wait_ge(prep_done, n + 1)
                bank = ps[:, n % PREP_BANKS, :]
                if kind == "rel":
                    nc.scalar.activation(far_bias[:], bank[:, NREL:NREL + 1], ACT.Identity, bias=k_bias[:])
                    last = copy(rel_rows[:], bank[0:RR, 0:NREL])
                elif kind == "gate_up":
                    last = copy((wgT, wuT)[a][:], bank[:, 0:HID])
                elif kind == "down":
                    last = copy(wdT[:], bank[:, 0:FT * P].rearrange("p (f d) -> p f d", f=FT))
                elif kind == "small":
                    copy(gateT[:], bank[:, 0:NE])
                    last = copy(b1T[:], bank[:, NE:NE + MF * NE].rearrange("p (m e) -> p m e", m=MF))
                elif kind == "w1":
                    last = copy(w1T[:, a, :], bank[:, :])
                else:
                    last = copy(w2T[:, :, a, :], bank[:, :].rearrange("p (m d) -> p m d", m=MF))
                last.then_inc((prep_act, prep_dve)[which], 1)

        def copies(n):
            return (n // 2 + 1, 0) if n % 2 == 0 else (0, n // 2 + 1)

        @block.scalar
        def _(act):
            def copy(o, i):
                return nc.scalar.activation(o, i, ACT.Copy)

            def head_copies(b, ahead):
                def proj(n):
                    act.wait_ge(head_proj_ps.sem, head_proj_ps.at(b, ahead * head_proj_ps.per + n))
                act.wait_ge(head_xT_ps.sem, head_xT_ps.at(b, ahead + 1))
                copy(head_T[:], ps[:, 6, :]).then_inc(head_xT.sem, 1)
                yield
                proj(1)
                nc.scalar.activation(qT[:], ps[:, 7, :], ACT.Identity, bias=q_bias[:]).then_inc(head_proj.sem, 1)
                proj(2)
                nc.scalar.activation(kT[:], ps[:, 6, :], ACT.Identity, bias=k_bias[:]).then_inc(head_proj.sem, 1)
                nc.scalar.activation(kT_far[:], ps[:, 6, :], ACT.Identity, bias=far_bias[:]
                                     ).then_inc(head_proj.sem, 1)
                yield
                proj(3)
                copy(v_ones[:, :, :, 0:D], ps[:, 7, :].rearrange("p (t h d) -> p t h d", t=T, d=D)
                     ).then_inc(head_proj.sem, 1)
                yield

            act.wait_ge(ld_attn, 9 * 16)
            act.wait_ge(consts_early, 1)
            prep_copy(act, copy, 0, end=1)
            act.wait_ge(toep_base, 2)
            for i in range(QB):
                c = S - QB - NREL + 1 + i
                act.dma_start(toep[i * D:(i + 1) * D, c:c + NREL],
                              rel_rows[i * D:(i + 1) * D, :]).then_inc(toep_dma, 16)
            act.wait_ge(prep_act, 1)
            for _ in head_copies(0, 0):
                pass
            act.wait_ge(j_ready, 1)
            nc.scalar.activation(j_turn[:], j_row[:], ACT.Sin, accum_out=j_sum[:]).then_inc(j_ready, 1)
            prep_copy(act, copy, 0, first=1)
            act.wait_ge(consts_ready, 1)
            act.wait_ge(j_ready, 3)
            nc.scalar.mul(j_bias[:], ps[:, 7, 0:1], 0.1 / E).then_inc(j_ready, 1)
            nc.scalar.activation(qbias_col[:], ps[:, 7, 2:4], ACT.Copy).then_inc(j_ready, 1)

            with act.Fori(0, B) as b:
                def transposed(k):
                    act.wait_ge(xnT_ps.sem, xnT_ps.at(b, k + 1))
                    nc.scalar.activation(xnT[:], ps[:, 6, :], ACT.Copy).then_inc(xnT_ready.sem, 1)

                nc.scalar.preload_act_table_set("exp_and_others")
                act.wait_ge(probs_zero.sem, probs_zero.at(b, 1))

                def copy_pT(n):
                    act.wait_ge(pT_ps.sem, pT_ps.at(b, n + 1))
                    t, c = n // QPT, n // QPT + 1
                    if t >= 2:
                        act.wait_ge(av_ps.sem, av_ps.at(b, t - 1))
                    if n == 2 * QPT + 1:
                        act.wait_ge(x_stored.sem, x_stored.at(b, 0))
                    nc.scalar.activation(
                        probsT[t % 2][:, 0:c, :, (n % QPT) * QB:(n % QPT + 1) * QB],
                        ps[:, 4 + n % 2, 0:c * P].rearrange("p (c h i) -> p c h i", h=H, i=QB),
                        ACT.Copy).then_inc(pT_act.sem, 1)

                def copy_attnT(t):
                    act.wait_ge(attnT_ps.sem, attnT_ps.at(b, t + 1))
                    nc.scalar.activation(attnT[:, t * P:(t + 1) * P], ps[:, 6, 256:256 + P], ACT.Copy
                                         ).then_inc(attnT_ready.sem, 1)

                for n in range(NQB):
                    act.wait_ge(max_ready.sem, max_ready.at(b, n + 1))
                    if n >= NB:
                        act.wait_ge(pT_ps.sem, pT_ps.at(b, n - NB + 1))
                    L = QB * (n + 1)
                    nc.scalar.activation(probs[:, n % NB, 0:L], ps[:, n % NB, 0:L], ACT.Exp,
                                         bias=neg_max[:, n % 8:n % 8 + 1]).then_inc(exp_ready.sem, 1)
                    if n >= 2 and (n - 2) % 2:
                        copy_pT(n - 2)
                    if n >= QPT and n % QPT == 9:
                        copy_attnT(n // QPT - 1)
                copy_pT(NQB - 1)
                copy_attnT(T - 1)

                transposed(0)
                for f in range(FT):
                    act.wait_ge(gu_ps.sem, gu_ps.at(b, 2 * f + 1))
                    nc.scalar.activation(hid_e[:, f, :], ps[:, f, :], ACT.Tanh, scale=0.5
                                         ).then_inc(ge_ready.sem, 1)

                nc.scalar.preload_act_table_set("natural_log_exp_and_others")
                transposed(1)
                for w in range(2):
                    act.wait_ge(proj_ps.sem, proj_ps.at(b, w + 1))
                    nc.scalar.activation(lin[:, w, :], ps[:, w, :], ACT.Identity,
                                         bias=qbias_col[:, w:w + 1]).then_inc(proj_copied.sem, 1)
                    nc.scalar.activation(lin_sq[:, w, :], ps[:, w, :], ACT.Square,
                                         bias=qbias_col[:, w:w + 1]).then_inc(proj_copied.sem, 1)
                act.wait_ge(proj_ps.sem, proj_ps.at(b, 3))
                nc.scalar.activation(v_ones[:, :, :, 0:D],
                                     ps[:, 2, :].rearrange("p (t h d) -> p t h d", t=T, d=D),
                                     ACT.Copy).then_inc(proj_copied.sem, 1)
                for w in range(2):
                    act.wait_ge(norm_ps.sem, norm_ps.at(b, w + 1))
                    nc.scalar.activation(lin_sq[:, w, :], ps[:, 3 + w, :], ACT.Ln, bias=eps_col[:]
                                         ).then_inc(act_step.sem, 1)
                for w in range(2):
                    act.wait_ge(act_step.sem, act_step.at(b, w + 1))
                    nc.scalar.activation(lin_sq[:, w, :], lin_sq[:, w, :], ACT.Exp, scale=-0.5
                                         ).then_inc(qnorm_ready.sem, 1)
                act.wait_ge(halves_ready.sem, halves_ready.at(b, 1))
                for c in range(4):
                    last = copy(k_parts[c * GR:(c + 1) * GR, 0, :], halves[0:GR, c // 2, :].bitcast(f32))
                last.then_inc(k_first_ready.sem, 1)
                for n in range(2 * HG):
                    for g in range(GH):
                        i = n * GH + g
                        act.wait_ge(s2_ready.sem, s2_ready.at(b, i + 1))
                        if n >= 2 and g == 0:
                            act.wait_ge(av2_ps.sem, av2_ps.at(b, n - 1))
                        nc.scalar.activation(head_probs[:, n % 2, g, :, :],
                                             ps[:, 2 * (i % 2):2 * (i % 2) + 2, :], ACT.Exp, bias=j_bias[:]
                                             ).then_inc(e2_ready.sem, 1)
                act.wait_ge(attnT_ps.sem, attnT_ps.at(b, T + 1))
                nc.scalar.activation(attnT[:], ps[:, 6, :], ACT.Copy).then_inc(attnT_ready.sem, 1)

                transposed(2)
                act.wait_ge(router_in.sem, router_in.at(b, 1))
                nc.scalar.activation(router_e[:], router[:], ACT.Exp).then_inc(router_exp.sem, 1)
                nc.scalar.preload_act_table_set("gelu_apprx_tanh_and_others")
                act.wait_ge(gatesT_ps.sem, gatesT_ps.at(b, 1))
                nc.scalar.activation(gates_T[:], ps[0:NE, 7, :].rearrange("p (t s) -> p t s", t=T), ACT.Copy
                                     ).then_inc(gatesT_ready.sem, 1)
                copies_ahead = head_copies(b, 1)
                for e in range(NE):
                    if 2 <= e < 5:
                        next(copies_ahead)
                    for m in range(MF):
                        n = e * MF + m
                        act.wait_ge(moe_h_ps.sem, moe_h_ps.at(b, n + 1))
                        if e >= 2 and m == 0:
                            act.wait_ge(moe_y_ps.sem, moe_y_ps.at(b, e - 1))
                        nc.scalar.activation(moe_h[:, e % 2, m, :], ps[:, n % NB, :], ACT.Gelu_apprx_tanh,
                                             bias=b1T[:, m, e:e + 1]).then_inc(moe_h_ready.sem, 1)

        @block.vector
        def _(dve):
            chain = [0]

            def prep(ins):
                chain[0] += 1
                ins.then_inc(prep_chain, 1)
                dve.wait_ge(prep_chain, chain[0])

            dve.wait_ge(consts_early, 1)
            dve.wait_ge(ld_attn, 9 * 16)
            nc.vector.tensor_copy(rel_first, rel_in[:, 0:1, :].broadcast_to([P, H, D])).then_inc(rep_ready, 1)
            nc.vector.tensor_copy(rel_rep, rel_in[:].unsqueeze(2).broadcast_to([P, NREL // P, QB, D])
                                  ).then_inc(rep_ready, 1)
            for z in range(2):
                nc.vector.tensor_copy(wq_rep[:, :, z, :, :],
                                      w_qkvo[:, 0, :].rearrange("p (c z d) -> p c z d", z=2, d=D)[:, :, z, :]
                                      .unsqueeze(2).broadcast_to([P, H // 2, QB, D])).then_inc(rep_ready, 1)
            dve.wait_ge(prep_act, 1)
            nc.vector.tensor_copy(toep[0:RR, 0:NREL], rel_rows[:, 0:1].broadcast_to([RR, NREL])
                                  ).then_inc(toep_base, 1)
            nc.vector.tensor_copy(toep[0:RR, NREL:S], rel_rows[:, NREL - 1:NREL].broadcast_to([RR, S - NREL])
                                  ).then_inc(toep_base, 1)
            def carry_wait():
                nc.vector.tensor_copy(spare[:, 0:1], ident[:, 0:1])

            def moments_of(src, step, mv, rs):
                for t in range(T):
                    last = nc.vector.bn_stats(stats[:, t, :], src[:, t, :])
                step(last)
                carry_wait()
                for t in range(T):
                    last = nc.vector.bn_aggr(mv[:, t, :], stats[:, t, :])
                step(last)
                v, y, z = root[:, 0, :], root[:, 1, :], root[:, 2, :]
                step(nc.vector.tensor_scalar(v, mv[:, :, 1], LN_EPS, None, ALU.add))
                step(nc.vector.tensor_scalar(y.bitcast(i32), v.bitcast(i32), -0.5, float(0x5f3759df),
                                             ALU.mult, ALU.add))
                c = (3.0 / 8.0) ** 0.5
                step(nc.vector.scalar_tensor_tensor(out=z, in0=y, scalar=c, in1=y, op0=ALU.mult, op1=ALU.mult))
                step(nc.vector.tensor_tensor(out=z, in0=z, in1=v, op=ALU.mult))
                step(nc.vector.scalar_tensor_tensor(out=z, in0=z, scalar=-1.25 / c, in1=z,
                                                    op0=ALU.add, op1=ALU.mult))
                step(nc.vector.scalar_tensor_tensor(out=y, in0=z, scalar=15.0 / 8.0, in1=y,
                                                    op0=ALU.add, op1=ALU.mult))
                step(nc.vector.scalar_tensor_tensor(out=z, in0=y, scalar=-0.5, in1=y,
                                                    op0=ALU.mult, op1=ALU.mult))
                step(nc.vector.tensor_tensor(out=z, in0=z, in1=v, op=ALU.mult))
                step(nc.vector.scalar_tensor_tensor(out=rs, in0=z, scalar=1.5, in1=y,
                                                    op0=ALU.add, op1=ALU.mult))

            def head(b, ahead):
                count = [0]

                def step(ins):
                    count[0] += 1
                    ins.then_inc(head_step.sem, 1)
                    dve.wait_ge(head_step.sem, head_step.at(b, ahead * head_step.per + count[0]))

                dve.wait_ge(x_loaded.sem, x_loaded.at(b, 16 * (ahead + 1)))
                moments_of(x_in, step, moments, rstd[:])
                for t in range(T):
                    nc.vector.tensor_scalar(xn[:, t, :], x_in[:, t, :], moments[:, t, 0:1], rstd[:, t:t + 1],
                                            ALU.subtract, ALU.mult).then_inc(head_xn.sem, 1)
                assert count[0] == head_step.per, count[0]
                yield
                if not ahead:
                    dve.wait_ge(ld_bias, 2 * QB * 16)
                for c in range(H // 2):
                    dve.wait_ge(qrel_ps.sem, qrel_ps.at(b, ahead * qrel_ps.per + c + 1))
                    for hh in range(2):
                        rows = slice(hh * RR, (hh + 1) * RR)
                        last = nc.vector.scalar_tensor_tensor(
                            out=q_rel[0:RR, :, 2 * c + hh, :],
                            in0=ps[rows, 6 + c % 2, :].rearrange("p (n i) -> p n i", i=QB),
                            scalar=q_bias_rep[rows, c:c + 1],
                            in1=query_mask[rows, :].unsqueeze(1).broadcast_to([RR, NQB, QB]),
                            op0=ALU.add, op1=ALU.mult)
                    last.then_inc(qrel_ready.sem, 1)
                    yield

            first_head = head(0, 0)
            next(first_head)
            nc.vector.tensor_copy(q_rel[RR:RR + QB, :, :, :].rearrange("p n h i -> p (n h) i"),
                                  ident[RR:RR + QB, RR:RR + QB].unsqueeze(1).broadcast_to([QB, NQB * H, QB])
                                  ).then_inc(rep_ready, 1)
            dve.wait_ge(ld_rows, 5 * 16)
            SIGN = {0: "+---", 1: "+++-", 2: "+-++", 3: "++-+"}
            for w in range(1, 4):
                for part in range(4):
                    src = qbias_in[:, :, 0, :] if w == 1 else qbias_row[:, :, part, :]
                    ins = nc.vector.tensor_tensor(out=qbias_row[:, :, part, :], in0=src,
                                                  in1=qbias_in[:, :, w, :],
                                                  op=ALU.add if SIGN[part][w] == "+" else ALU.subtract)
                    if w < 3:
                        prep(ins)
                    else:
                        ins.then_inc(qb_ready, 1)
            BIG = 1.5 * 2.0 ** 23
            c1 = 6.28125
            c2 = float(np.float32(TWO_PI - c1))
            prep(nc.vector.tensor_scalar(j_turn[:], j_row[:], 1.0 / TWO_PI, BIG, ALU.mult, ALU.add))
            prep(nc.vector.tensor_scalar(j_turn[:], j_turn[:], BIG, None, ALU.subtract))
            prep(nc.vector.scalar_tensor_tensor(out=j_row[:], in0=j_turn[:], scalar=-c1, in1=j_row[:],
                                                op0=ALU.mult, op1=ALU.add))
            prep(nc.vector.scalar_tensor_tensor(out=j_row[:], in0=j_turn[:], scalar=-c2, in1=j_row[:],
                                                op0=ALU.mult, op1=ALU.add))
            PI_IN = float(np.nextafter(np.float32(np.pi), np.float32(0)))
            nc.vector.tensor_scalar(j_row[:], j_row[:], PI_IN, -PI_IN, ALU.min, ALU.max).then_inc(j_ready, 1)
            for _ in first_head:
                pass
            dve.wait_ge(ld_ffn, 3 * 16)
            nc.vector.tensor_scalar(wf_in, wi_in, DEQ, None, ALU.mult).then_inc(wf_ready, 1)
            prep_copy(dve, lambda o, i: nc.vector.tensor_copy(o, i), 1)
            dve.wait_ge(ld_quat, 4 * 9 * 16)
            dve.wait_ge(consts_ready, 1)
            for m in range(4):
                nc.vector.tensor_tensor(out=w_quat[:, m, :, :], in0=w_quat[:, m, :, :],
                                        in1=signs[:].unsqueeze(2).broadcast_to([P, 4, QD]),
                                        op=ALU.mult).then_inc(qb_ready, 1)
            dve.wait_ge(j_ready, 5)
            nc.vector.memset(spare[:, 1:2], 0.0).then_inc(x_copied.sem, 1)
            nc.vector.memset(spare[:, 2:3], 0.0).then_inc(x_final.sem, 1)
            nc.vector.memset(spare[:, 3:4], 0.0).then_inc(x_stored.sem, 16)

            with dve.Fori(0, B) as b:
                count = [0]

                def step(ins):
                    count[0] += 1
                    ins.then_inc(dve_step.sem, 1)
                    dve.wait_ge(dve_step.sem, dve_step.at(b, count[0]))

                def norm_in(k):
                    dve.wait_ge(y_ready.sem, y_ready.at(b, k + 1))
                    moments_of(y_bank, step, y_moments, y_rstd[:])
                    for t in range(T):
                        last = nc.vector.scalar_tensor_tensor(out=x[:, t, :], in0=y_bank[:, t, :],
                                                              scalar=y_rstd[:, t:t + 1], in1=x[:, t, :],
                                                              op0=ALU.mult, op1=ALU.add)
                    step(last)
                    moments_of(x, step, moments, rstd[:])
                    for t in range(T):
                        nc.vector.tensor_scalar(xn[:, t, :], x[:, t, :], moments[:, t, 0:1], rstd[:, t:t + 1],
                                                ALU.subtract, ALU.mult).then_inc(xn_ready.sem, 1)
                    dve.wait_ge(xn_ready.sem, xn_ready.at(b, (k + 1) * T))
                    step(nc.vector.tensor_tensor(out=y_rstd[:], in0=y_rstd[:], in1=y_moments[:, :, 0],
                                                 op=ALU.mult))
                    step(nc.vector.tensor_tensor(out=x[:], in0=x[:],
                                                 in1=y_rstd[:].unsqueeze(2).broadcast_to([P, T, E]),
                                                 op=ALU.subtract))

                y_bank = ps[:, 7, :].rearrange("p (t e) -> p t e", t=T)


                def copy_pT(n):
                    dve.wait_ge(pT_ps.sem, pT_ps.at(b, n + 1))
                    t, c = n // QPT, n // QPT + 1
                    if t >= 2:
                        dve.wait_ge(av_ps.sem, av_ps.at(b, t - 1))
                    if n == 2 * QPT:
                        dve.wait_ge(x_stored.sem, x_stored.at(b, 0))
                    nc.vector.tensor_copy(
                        probsT[t % 2][:, 0:c, :, (n % QPT) * QB:(n % QPT + 1) * QB],
                        ps[:, 4 + n % 2, 0:c * P].rearrange("p (c h i) -> p c h i", h=H, i=QB)
                    ).then_inc(pT_dve.sem, 1)

                def copy_outT(n, av, count):
                    dve.wait_ge(av.sem, av.at(b, count))
                    nc.vector.tensor_copy(outT[:], ps[:, (6 if n < T else 4 + n % 2), :]
                                          ).then_inc(outT_ready.sem, 1)

                def divide_out(n, dst, slots):
                    dve.wait_ge(turned_ps.sem, turned_ps.at(b, n + 1))
                    o = ps[:, 6, :].rearrange("p (k g r) -> p k g r", k=4, g=GH)
                    step(nc.vector.reciprocal(slots, o[:, :, :, D]))
                    nc.vector.tensor_tensor(out=dst, in0=o[:, :, :, 0:D],
                                            in1=slots.unsqueeze(3).broadcast_to([P, 4, GH, D]),
                                            op=ALU.mult).then_inc(attn_ready.sem, 1)

                def divide_tile(t):
                    divide_out(t, attn[:, t, :].rearrange("p (k g d) -> p k g d", g=GH, d=D),
                               den[:, t, :].rearrange("p (k g) -> p k g", g=GH))

                for n in range(NQB):
                    if n == QPT // 2:
                        dve.wait_ge(x_final.sem, x_final.at(b, 0))
                        nc.vector.tensor_copy(x[:], x_in[:]).then_inc(x_copied.sem, 1)
                    dve.wait_ge(scores_ready.sem, scores_ready.at(b, n + 1))
                    if n >= 8:
                        dve.wait_ge(exp_ready.sem, exp_ready.at(b, n - 7))
                    nc.vector.tensor_reduce(neg_max[:, n % 8:n % 8 + 1], ps[:, n % NB, 0:QB * (n + 1)],
                                            axis=AXX, op=ALU.max, negate=True).then_inc(max_ready.sem, 1)
                    if n >= 3 and (n - 3) % 2 == 0:
                        copy_pT(n - 3)
                    if n == QPT + 5:
                        dve.wait_ge(qwide_ready.sem, qwide_ready.at(b, T))
                    if n >= QPT and n % QPT == 5:
                        copy_outT(n // QPT - 1, av_ps, n // QPT)
                    if n >= QPT and n % QPT == 7:
                        divide_tile(n // QPT - 1)
                copy_pT(NQB - 2)
                copy_outT(T - 1, av_ps, T)
                divide_tile(T - 1)

                dve.wait_ge(x_copied.sem, x_copied.at(b, 1))

                norm_in(0)
                for f in range(FT):
                    dve.wait_ge(ge_ready.sem, ge_ready.at(b, f + 1))
                    step(nc.vector.scalar_tensor_tensor(out=hid_e[:, f, :], in0=hid_e[:, f, :], scalar=1.0,
                                                        in1=ps[:, f, :], op0=ALU.add, op1=ALU.mult))
                    dve.wait_ge(gu_ps.sem, gu_ps.at(b, 2 * f + 2))
                    nc.vector.scalar_tensor_tensor(out=hid[:, f, :], in0=hid_e[:, f, :], scalar=0.5,
                                                   in1=ps[:, 3 + f, :], op0=ALU.mult, op1=ALU.mult
                                                   ).then_inc(hid_ready.sem, 1)

                norm_in(1)
                for w in range(2):
                    dve.wait_ge(qnorm_ready.sem, qnorm_ready.at(b, w + 1))
                    nc.vector.tensor_tensor(out=(qT, kT)[w][:], in0=lin[:, w, :], in1=lin_sq[:, w, :],
                                            op=ALU.mult).then_inc(qk_ready.sem, 1)
                dve.wait_ge(qk_ready.sem, qk_ready.at(b, 2))
                for w, src in enumerate((kT, qT)):
                    step(nc.vector.tensor_copy(halves[:, 2 * w, :], src[:]))
                    low = nc.vector.tensor_tensor(out=halves[:, 2 * w + 1, :], in0=src[:],
                                                  in1=halves[:, 2 * w, :].bitcast(f32), op=ALU.subtract)
                    if w == 0:
                        low.then_inc(halves_ready.sem, 1)
                    else:
                        step(low)

                def spread_q(hg):
                    for c in range(4):
                        last = nc.vector.tensor_copy(q_parts[c * GR:(c + 1) * GR, hg, :],
                                                     halves[hg * GR:(hg + 1) * GR, 2 + c % 2, :].bitcast(f32))
                    last.then_inc(q_parts_ready.sem, 1)

                def mask_heads(hg):
                    dve.wait_ge(q_parts_ready.sem, q_parts_ready.at(b, hg + 1 if hg == 0 else HG))
                    if hg == 1:
                        dve.wait_ge(k_first_ready.sem, k_first_ready.at(b, 1))
                        dve.wait_ge(k_rest_ready.sem, k_rest_ready.at(b, k_rest_ready.per))
                    if hg >= 2:
                        dve.wait_ge(s2_ready.sem, s2_ready.at(b, 2 * GH * (hg - 1)))
                    for g in range(GH):
                        nc.vector.tensor_scalar(q_heads[:, hg % 2, g, :], q_parts[:, hg, :].bitcast(f32),
                                                group_mask[:, g:g + 1], None, ALU.mult
                                                ).then_inc(q_heads_ready.sem, 1)

                spread_q(0)
                mask_heads(0)
                for hg in range(1, HG):
                    spread_q(hg)
                mask_heads(1)
                for hg in range(HG):
                    copy_outT(T + hg, av2_ps, 2 * hg + 2)
                    if hg + 2 < HG:
                        mask_heads(hg + 2)
                    divide_out(T + hg, attn[:].rearrange("p t (k g d) -> p t k g d", g=GH, d=D)[:, :, hg, :, :],
                               den[:].rearrange("p t (k g) -> p t k g", g=GH)[:, :, hg, :])

                norm_in(2)
                dve.wait_ge(router_ps.sem, router_ps.at(b, 1))
                lg = ps[:, 6, 0:T * NE].rearrange("p (t e) -> p t e", t=T)

                def per_token(a):
                    return a.broadcast_to([P, T, NE])

                step(nc.vector.tensor_reduce(router_s[:, :, 0], lg, axis=AXX, op=ALU.max, negate=True))
                nc.vector.tensor_tensor(out=router[:], in0=lg, in1=per_token(router_s[:, :, 0:1]), op=ALU.add
                                        ).then_inc(router_in.sem, 1)
                dve.wait_ge(router_exp.sem, router_exp.at(b, 1))
                step(nc.vector.tensor_reduce(router_s[:, :, 1], router_e[:], axis=AXX, op=ALU.add))
                step(nc.vector.reciprocal(router_s[:, :, 0], router_s[:, :, 1]))
                step(nc.vector.tensor_tensor(out=router[:], in0=router_e[:], in1=per_token(router_s[:, :, 0:1]),
                                             op=ALU.mult))
                carry_wait()
                for t in range(T):
                    last = nc.vector.max(top8[:, t, :], router[:, t, :])
                step(last)
                carry_wait()
                for t in range(T):
                    last = nc.vector.max_index(top_idx[:, t, :], top8[:, t, :], router[:, t, :])
                step(last)
                step(nc.vector.tensor_copy(top_idx_f[:], top_idx[:]))
                numbers = expert_no[:].unsqueeze(1).broadcast_to([P, T, NE])
                for j, g in enumerate((gates, gates2)):
                    step(nc.vector.tensor_tensor(out=g[:], in0=numbers, in1=per_token(top_idx_f[:, :, j:j + 1]),
                                                 op=ALU.is_equal))
                    step(nc.vector.tensor_tensor(out=g[:], in0=g[:], in1=per_token(top8[:, :, j:j + 1]),
                                                 op=ALU.mult))
                nc.vector.tensor_tensor(out=gates[:], in0=gates[:], in1=gates2[:], op=ALU.add
                                        ).then_inc(gates_ready.sem, 1)
                ahead = head(b, 1)
                next(ahead)
                dve.wait_ge(accb_ps.sem, accb_ps.at(b, 1))
                nc.vector.tensor_copy(acc, y_bank).then_inc(acc_ready.sem, 1)
                dve.wait_ge(acc_ready.sem, acc_ready.at(b, 1))
                for e in range(NE):
                    if 3 <= e < 7:
                        next(ahead)
                        next(ahead)
                    dve.wait_ge(moe_y_ps.sem, moe_y_ps.at(b, e + 1))
                    for t in range(T):
                        last = nc.vector.scalar_tensor_tensor(
                            out=acc[:, t, :], in0=ps[:, 4 + e % 2, t * P:(t + 1) * P],
                            scalar=gates[:, t, e:e + 1], in1=acc[:, t, :], op0=ALU.mult, op1=ALU.add)
                    last.then_inc(moe_y_used.sem, 1)
                    dve.wait_ge(moe_y_used.sem, moe_y_used.at(b, e + 1))
                moments_of(acc, step, moments, rstd[:])
                for t in range(T):
                    last = nc.vector.tensor_scalar(y_out[:, t, :], acc[:, t, :], moments[:, t, 0:1],
                                                   rstd[:, t:t + 1], ALU.subtract, ALU.mult)
                step(last)
                nc.vector.tensor_tensor(out=x_out, in0=x[:], in1=y_out, op=ALU.add).then_inc(x_final.sem, 1)
                assert count[0] == dve_step.per, count[0]

        @block.tensor
        def _(pe):
            mm = nc.tensor.matmul
            pe.wait_ge(consts_early, 1)

            def head(b, ahead):
                for t in range(T):
                    pe.wait_ge(head_xn.sem, head_xn.at(b, ahead * T + t + 1))
                    last = nc.tensor.transpose(ps[:, 6, t * P:(t + 1) * P], xn[:, t, :], ident[:])
                last.then_inc(head_xT_ps.sem, 1)
                yield
                pe.wait_ge(head_xT.sem, head_xT.at(b, ahead + 1))
                if ahead:
                    pe.wait_ge(acc_ready.sem, acc_ready.at(b, 1))
                mm(ps[:, 7, :], w_qkvo[:, 0, :], head_T[:], start=True, stop=True).then_inc(head_proj_ps.sem, 1)
                mm(ps[:, 6, :], w_qkvo[:, 1, :], head_T[:], start=True, stop=True).then_inc(head_proj_ps.sem, 1)
                yield
                pe.wait_ge(head_proj.sem, head_proj.at(b, ahead * head_proj.per + 1))
                for t in range(T):
                    last = token_major(7, t, w_qkvo[:, 2, :], bias_rows[:, 0, :], head_T)
                last.then_inc(head_proj_ps.sem, 1)
                yield
                for c in range(H // 2):
                    if c < 2:
                        pe.wait_ge(head_proj.sem, head_proj.at(b, ahead * head_proj.per + 3 + c))
                    else:
                        pe.wait_ge(qrel_ready.sem, qrel_ready.at(b, ahead * qrel_ready.per + c - 1))
                    mm(ps[:, 6 + c % 2, :], wq_rep[:, c, :, :, :], head_T[:], start=True, stop=True
                       ).then_inc(qrel_ps.sem, 1)
                    if c % 2:
                        yield

            def token_major(bank, t, w, bias, src):
                o = ps[:, bank, t * P:(t + 1) * P]
                mm(o, src[:, t * P:(t + 1) * P], w, start=True, stop=False)
                return mm(o, ones[:], bias, start=False, stop=True)

            for n, (kind, a) in enumerate(groups):
                if n == 0:
                    pe.wait_ge(ld_attn, 9 * 16)
                    pe.wait_ge(rep_ready, 4)
                if n == 1:
                    for _ in head(0, 0):
                        pass
                    pe.wait_ge(wf_ready, 1)
                if n == first_moe:
                    pe.wait_ge(ld_moe, 5 * 16)
                if n >= PREP_BANKS:
                    ca, cd = copies(n - PREP_BANKS)
                    if ca:
                        pe.wait_ge(prep_act, ca)
                    if cd:
                        pe.wait_ge(prep_dve, cd)
                bank = ps[:, n % PREP_BANKS, :]
                if kind == "rel":
                    for c in range(NREL // P):
                        last = mm(bank[0:RR, c * P:(c + 1) * P],
                                  rel_rep[:, c, :, :], ident[:], start=True, stop=True)
                    last = mm(bank[:, NREL:NREL + 1], rel_first, ident[:, 0:1], start=True, stop=True)
                elif kind in ("gate_up", "down"):
                    for f in range(FT):
                        last = nc.tensor.transpose(bank[:, f * P:(f + 1) * P],
                                                   wf_in[:, a, f * P:(f + 1) * P], ident[:])
                elif kind == "small":
                    nc.tensor.transpose(bank[:, 0:NE], gate_in, ident[0:NE, 0:NE])
                    for m in range(MF):
                        last = nc.tensor.transpose(bank[:, NE * (m + 1):NE * (m + 2)],
                                                   b1_in[:, m * P:(m + 1) * P], ident[0:NE, 0:NE])
                elif kind == "w1":
                    for m in range(MF):
                        last = nc.tensor.transpose(bank[:, m * P:(m + 1) * P], w1_in[:, m, a, :], ident[:])
                else:
                    for m in range(MF):
                        last = nc.tensor.transpose(bank[:, m * P:(m + 1) * P],
                                                   w2_in[:, a, m * P:(m + 1) * P], ident[:])
                last.then_inc(prep_done, 1)
            pe.wait_ge(prep_act, (len(groups) + 1) // 2)
            pe.wait_ge(prep_dve, len(groups) // 2)
            pe.wait_ge(j_ready, 2)
            pe.wait_ge(qb_ready, 8)
            row = qbias_row[:].rearrange("a m c o -> a m (c o)")
            for m in range(2):
                mm(ps[:, 7, 2 + m:3 + m], row[:, m, :], ones[:, 0:1], start=True, stop=True)
            mm(ps[:, 7, 0:1], ones[:], j_sum[:], start=True, stop=True).then_inc(j_ready, 1)
            pe.wait_ge(j_ready, 5)
            pe.wait_ge(toep_dma, 16 * QB)
            pe.wait_ge(consts_ready, 1)

            with pe.Fori(0, B) as b:
                def input_T(k):
                    for t in range(T):
                        pe.wait_ge(xn_ready.sem, xn_ready.at(b, k * T + t + 1))
                        last = nc.tensor.transpose(ps[:, 6, t * P:(t + 1) * P], xn[:, t, :], ident[:])
                    last.then_inc(xnT_ps.sem, 1)
                    pe.wait_ge(xnT_ready.sem, xnT_ready.at(b, k + 1))

                pe.wait_ge(qrel_ready.sem, qrel_ready.at(b, H // 2))
                pe.wait_ge(head_proj.sem, head_proj.at(b, head_proj.per))

                def scores(n):
                    if n % QPT == 0:
                        pe.wait_ge(qwide_ready.sem, qwide_ready.at(b, n // QPT + 1))
                    if n >= NB:
                        pe.wait_ge(exp_ready.sem, exp_ready.at(b, n - NB + 1))
                    L = QB * (n + 1)
                    near = max(0, L - QB - NREL + 2)
                    if near:
                        mm(ps[:, n % NB, 0:near], q_wide0[:, n, :, :], kT_far[:, 0:near], start=True, stop=True,
                           skip_group_check=True)
                    o = ps[:, n % NB, near:L]
                    mm(o, q_wide0[:, n, :, :], kT[:, near:L], start=(not near), stop=False,
                       skip_group_check=True)
                    mm(o, q_rel[:, n, :, :], toep[:, S - L + near:S], start=False, stop=True,
                       skip_group_check=True).then_inc(scores_ready.sem, 1)

                def transpose_probs(n):
                    pe.wait_ge(exp_ready.sem, exp_ready.at(b, n + 1))
                    if n >= 2:
                        done = (pT_dve, pT_act)[n % 2]
                        pe.wait_ge(done.sem, done.at(b, n // 2))
                    for c in range(n // QPT + 1):
                        last = nc.tensor.transpose(ps[:, 4 + n % 2, c * P:(c + 1) * P],
                                                   probs[:, n % NB, c * P:(c + 1) * P], ident[:])
                    last.then_inc(pT_ps.sem, 1)

                def weigh_values(t):
                    pe.wait_ge(pT_dve.sem, pT_dve.at(b, (t + 1) * QPT // 2))
                    pe.wait_ge(pT_act.sem, pT_act.at(b, (t + 1) * QPT // 2))
                    for k in range(HG):
                        for c in range(t + 1):
                            for g in range(GH):
                                h = k * GH + g
                                last = mm(ps[32 * g:32 * g + D + 1, 6, k * P:(k + 1) * P],
                                          v_ones[:, c, h, :], probsT[t % 2][:, c, h, :],
                                          start=(c == 0), stop=(c == t))
                    last.then_inc(av_ps.sem, 1)

                def turn_out(n):
                    pe.wait_ge(outT_ready.sem, outT_ready.at(b, n + 1))
                    if n > T:
                        pe.wait_ge(attn_ready.sem, attn_ready.at(b, n))
                    for k in range(4):
                        last = nc.tensor.transpose(ps[:, 6, k * P:(k + 1) * P], outT[:, k * P:(k + 1) * P],
                                                   ident[:])
                    last.then_inc(turned_ps.sem, 1)

                def attn_T(t):
                    pe.wait_ge(attn_ready.sem, attn_ready.at(b, t + 1))
                    nc.tensor.transpose(ps[:, 6, 256:256 + P], attn[:, t, :], ident[:]
                                        ).then_inc(attnT_ps.sem, 1)

                def project(t):
                    pe.wait_ge(attnT_ready.sem, attnT_ready.at(b, t + 1))
                    return token_major(7, t, w_qkvo[:, 3, :], bias_rows[:, 1, :], attnT)

                for n in range(3):
                    scores(n)
                for n in range(NQB):
                    if n + 3 < NQB:
                        scores(n + 3)
                    transpose_probs(n)
                    t = n // QPT - 1
                    if t >= 0 and n % QPT == 3:
                        weigh_values(t)
                    if t >= 0 and n % QPT == 5:
                        turn_out(t)
                    if t >= 0 and n % QPT == 8:
                        attn_T(t)
                    if t >= 0 and n % QPT == 10:
                        project(t)
                weigh_values(T - 1)
                turn_out(T - 1)
                attn_T(T - 1)
                project(T - 1).then_inc(y_ready.sem, 1)

                input_T(0)
                for f in range(FT):
                    mm(ps[:, f, :], wgT[:, f * P:(f + 1) * P], xnT[:], start=True, stop=True
                       ).then_inc(gu_ps.sem, 1)
                    mm(ps[:, 3 + f, :], wuT[:, f * P:(f + 1) * P], xnT[:], start=True, stop=True
                       ).then_inc(gu_ps.sem, 1)
                pe.wait_ge(hid_ready.sem, hid_ready.at(b, FT))
                for t in range(T):
                    for f in range(FT):
                        last = mm(ps[:, 7, t * P:(t + 1) * P], hid[:, f, t * P:(t + 1) * P], wdT[:, f, :],
                                  start=(f == 0), stop=(f == FT - 1))
                last.then_inc(y_ready.sem, 1)

                input_T(1)
                wq2 = w_quat[:].rearrange("p m c o -> p m (c o)")
                for w in range(2):
                    mm(ps[:, w, :], wq2[:, w, :], xnT[:], start=True, stop=True).then_inc(proj_ps.sem, 1)
                for t in range(T):
                    last = token_major(2, t, wq2[:, 2, :], row[:, 2, :], xnT)
                last.then_inc(proj_ps.sem, 1)
                for w in range(2):
                    pe.wait_ge(proj_copied.sem, proj_copied.at(b, 2 * (w + 1)))
                    mm(ps[:, 3 + w, :], same_part[:], lin_sq[:, w, :], start=True, stop=True
                       ).then_inc(norm_ps.sem, 1)
                pe.wait_ge(proj_copied.sem, proj_copied.at(b, 5))
                pe.wait_ge(qk_ready.sem, qk_ready.at(b, 2))

                def scores2(n, g):
                    hg, a, i = n // 2, n % 2, n * GH + g
                    if n == 0 and g == 0:
                        pe.wait_ge(k_first_ready.sem, k_first_ready.at(b, 1))
                    elif a == 0 and g == 0:
                        pe.wait_ge(k_rest_ready.sem, k_rest_ready.at(b, 4 * hg))
                    if a == 0:
                        pe.wait_ge(q_heads_ready.sem, q_heads_ready.at(b, hg * GH + g + 1))
                    if i >= 2:
                        pe.wait_ge(e2_ready.sem, e2_ready.at(b, i - 1))
                    for c in range(2):
                        key = (2 * a + c) * P
                        last = mm(ps[:, 2 * (i % 2) + c, :], k_parts[:, hg, key:key + P],
                                  q_heads[:, hg % 2, g, :], start=True, stop=True)
                    last.then_inc(s2_ready.sem, 1)

                def weigh_values2(n, pieces=(0, 1)):
                    hg, a = n // 2, n % 2
                    if 0 in pieces:
                        pe.wait_ge(e2_ready.sem, e2_ready.at(b, (n + 1) * GH))
                        if hg >= 2 and a == 0:
                            pe.wait_ge(outT_ready.sem, outT_ready.at(b, T + hg - 1))
                    for c in pieces:
                        for g in range(GH):
                            last = mm(ps[32 * g:32 * g + D + 1, 4 + hg % 2, :], v_ones[:, 2 * a + c, hg * GH + g, :],
                                      head_probs[:, n % 2, g, c, :], start=(a == 0 and c == 0),
                                      stop=(a == 1 and c == 1))
                    if 1 in pieces:
                        last.then_inc(av2_ps.sem, 1)

                for n in range(2 * HG):
                    for g in range(GH):
                        scores2(n, g)
                        if g % 2 and n >= 1:
                            weigh_values2(n - 1, (g // 2,))
                        if g == 3 and n >= 3 and n % 2:
                            turn_out(T + n // 2 - 1)
                weigh_values2(2 * HG - 1)
                turn_out(T + HG - 1)
                for t in range(T):
                    pe.wait_ge(attn_ready.sem, attn_ready.at(b, T + HG))
                    last = nc.tensor.transpose(ps[:, 6, t * P:(t + 1) * P], attn[:, t, :], ident[:])
                last.then_inc(attnT_ps.sem, 1)
                pe.wait_ge(attnT_ready.sem, attnT_ready.at(b, T + 1))
                for t in range(T):
                    last = token_major(7, t, wq2[:, 3, :], row[:, 3, :], attnT)
                last.then_inc(y_ready.sem, 1)

                input_T(2)
                for t in range(T):
                    last = mm(ps[:, 6, t * NE:(t + 1) * NE], xnT[:, t * P:(t + 1) * P], gateT[:],
                              start=True, stop=True)
                last.then_inc(router_ps.sem, 1)

                def expert_up(e):
                    for m in range(MF):
                        n = e * MF + m
                        if n >= NB:
                            pe.wait_ge(moe_h_ready.sem, moe_h_ready.at(b, n - NB + 1))
                        mm(ps[:, n % NB, :], w1T[:, e, m * P:(m + 1) * P], xnT[:], start=True, stop=True
                           ).then_inc(moe_h_ps.sem, 1)

                def expert_down(e):
                    pe.wait_ge(moe_h_ready.sem, moe_h_ready.at(b, (e + 1) * MF))
                    if e >= 2:
                        pe.wait_ge(moe_y_used.sem, moe_y_used.at(b, e - 1))
                    for t in range(T):
                        for m in range(MF):
                            last = mm(ps[:, 4 + e % 2, t * P:(t + 1) * P],
                                      moe_h[:, e % 2, m, t * P:(t + 1) * P], w2T[:, m, e, :],
                                      start=(m == 0), stop=(m == MF - 1))
                    last.then_inc(moe_y_ps.sem, 1)

                expert_up(0)
                pe.wait_ge(gates_ready.sem, gates_ready.at(b, 1))
                for t in range(T):
                    last = nc.tensor.transpose(ps[0:NE, 7, t * P:(t + 1) * P], gates[:, t, :], ident[:])
                last.then_inc(gatesT_ps.sem, 1)
                pe.wait_ge(gatesT_ready.sem, gatesT_ready.at(b, 1))
                for t in range(T):
                    last = mm(ps[:, 7, t * P:(t + 1) * P], gates_T[:, t, :], b2_sb[:], start=True, stop=True)
                last.then_inc(accb_ps.sem, 1)
                pieces = head(b, 1)
                for e in range(NE):
                    if e + 1 < NE:
                        expert_up(e + 1)
                    if e < 7:
                        next(pieces)
                    expert_down(e)


_INS = ['L0_attn_x', 'L0_attn_Wq', 'L0_attn_bq', 'L0_attn_Wk', 'L0_attn_bk', 'L0_attn_Wv', 'L0_attn_bv',
        'L0_attn_Wo', 'L0_attn_bo', 'L0_attn_rel_key', 'L0_ffn_w_gate', 'L0_ffn_w_up', 'L0_ffn_w_down',
        'L1_attn_qW', 'L1_attn_qb', 'L1_attn_kW', 'L1_attn_kb', 'L1_attn_vW', 'L1_attn_vb', 'L1_attn_oW',
        'L1_attn_ob', 'L1_attn_J', 'L1_ffn_gate_w', 'L1_ffn_w1', 'L1_ffn_b1', 'L1_ffn_w2', 'L1_ffn_b2']


def kernel(**inputs):
    import numpy as _np
    import concourse.bacc as _bacc
    from concourse import mybir as _mybir
    from concourse.bass_utils import run_bass_kernel_spmd as _run

    nc = _bacc.Bacc("TRN2", target_bir_lowering=False, num_devices=1)
    arrays, args = {}, []
    for name in _INS:
        a = _np.ascontiguousarray(inputs[name])
        arrays[f"in_{name}_dram"] = a
        args.append(nc.dram_tensor(f"in_{name}_dram", a.shape, _mybir.dt.from_np(a.dtype), kind="ExternalInput").ap())
    shape = _np.shape(inputs['L0_attn_x'])
    o = nc.dram_tensor("out_dram", shape, _mybir.dt.float32, kind="ExternalOutput").ap()
    build_sandwich(nc, *args, o)
    r = _run(nc, [arrays], core_ids=[0])
    return r.results[0]["out_dram"]
```
